# Optimizing a Trainium2 kernel written in Bass

```python
import numpy as np
import jax
import jax.numpy as jnp

def _softmax(x, axis=-1):
    return jax.nn.softmax(x, axis=axis)

def _gelu(x):
    return jax.nn.gelu(x, approximate=True)

def _silu(x):
    return jax.nn.silu(x)

def _sigmoid(x):
    return jax.nn.sigmoid(x)

def _layernorm(x, axis=-1, eps=1e-05):
    m = jnp.mean(x, axis=axis, keepdims=True)
    v = jnp.var(x, axis=axis, keepdims=True)
    return (x - m) / jnp.sqrt(v + eps)

def _scatter_add(tgt, idx, src, axis=0):
    return tgt.at[idx].add(src)

def _segment_sum(src, seg, n):
    return jax.ops.segment_sum(src, seg, n)
kernel_name = 'mk_gnn_preln_d2_gnn_r64_901487'

def setup_inputs(seed: int=0):
    np.random.seed(seed)
    _w = jnp.asarray

    def _rec_inputs():
        import jax
        import jax.numpy as jnp
        _gk = jax.random.key(seed)
        x = -0.000202 + 1 * jax.random.normal(jax.random.fold_in(_gk, 1), (100000, 64), jnp.float32)
        src = jax.random.randint(jax.random.fold_in(_gk, 2), (50000,), 0, 100000, jnp.int32)
        dst = jax.random.randint(jax.random.fold_in(_gk, 3), (50000,), 0, 100000, jnp.int32)
        _o = jnp.argsort(dst, stable=True)
        src = src[_o]
        dst = dst[_o]
        edge_attr_64 = -5.72187e-05 + 0.999849 * jax.random.normal(jax.random.fold_in(_gk, 11), (50000, 64), jnp.float32)
        return (x, src, dst, edge_attr_64)
    x, src, dst, edge_attr_64 = _rec_inputs()

    def _L0_gnn_setup():
        import jax, jax.numpy as jnp
        import numpy as np
        N_NODES = 100000
        N_EDGES = 25000
        D = 64

        def _gcn_conv(x, src, dst, W, b, n_nodes):
            h = x @ W
            agg = jax.ops.segment_sum(h[src], dst, num_segments=n_nodes)
            return agg + b
        key = jax.random.key(seed)
        ks = jax.random.split(key, 6)
        v0 = jax.random.normal(ks[0], (N_NODES, D), dtype=jnp.float32)
        edge_index = jax.random.randint(ks[1], (2, N_EDGES), 0, N_NODES, dtype=jnp.int64)
        scale = 1.0 / np.sqrt(D)
        W1 = jax.random.normal(ks[2], (D, D), dtype=jnp.float32) * scale
        b1 = jnp.zeros((D,), dtype=jnp.float32)
        W2 = jax.random.normal(ks[3], (D, D), dtype=jnp.float32) * scale
        b2 = jnp.zeros((D,), dtype=jnp.float32)
        return {'v0': v0, 'edge_index': edge_index, 'W1': W1, 'b1': b1, 'W2': W2, 'b2': b2}
    _L0_gnn_all = _L0_gnn_setup()
    _L0_gnn_in = {k: v for k, v in _L0_gnn_all.items() if k in ('W1', 'b1', 'W2', 'b2')}
    del _L0_gnn_all

    def _L1_gnn_setup():
        import jax, jax.numpy as jnp
        import numpy as np
        N = 1024
        E = 16384
        F = 64
        NUM_AGGR = 4
        NUM_SCALER = 3
        EPS = 1e-05

        def _linear_init(key, fan_in, fan_out):
            kw, kb = jax.random.split(key)
            s = 1.0 / np.sqrt(fan_in)
            W = jax.random.uniform(kw, (fan_in, fan_out), jnp.float32, -s, s)
            b = jax.random.uniform(kb, (fan_out,), jnp.float32, -s, s)
            return (W, b)
        key = jax.random.key(seed)
        ks = jax.random.split(key, 8)
        x = jax.random.normal(ks[0], (N, F), jnp.float32)
        edge_attr = jax.random.normal(ks[1], (E, F), jnp.float32)
        edge_index = jax.random.randint(ks[2], (2, E), 0, N, dtype=jnp.int32)
        deg_hist = jnp.ones((32,), jnp.int32)
        W_e, b_e = _linear_init(ks[3], F, F)
        W_pre, b_pre = _linear_init(ks[4], 3 * F, F)
        W_post, b_post = _linear_init(ks[5], (NUM_AGGR * NUM_SCALER + 1) * F, F)
        W_lin, b_lin = _linear_init(ks[6], F, F)
        return {'x': x, 'edge_attr': edge_attr, 'edge_index': edge_index, 'deg_hist': deg_hist, 'W_e': W_e, 'b_e': b_e, 'W_pre': W_pre, 'b_pre': b_pre, 'W_post': W_post, 'b_post': b_post, 'W_lin': W_lin, 'b_lin': b_lin}
    _L1_gnn_all = _L1_gnn_setup()
    _L1_gnn_in = {k: v for k, v in _L1_gnn_all.items() if k in ('deg_hist', 'W_e', 'b_e', 'W_pre', 'b_pre', 'W_post', 'b_post', 'W_lin', 'b_lin')}
    del _L1_gnn_all
    return {'x': x, 'src': src, 'dst': dst, 'edge_attr_64': edge_attr_64, 'L0_gnn_W1': _L0_gnn_in['W1'], 'L0_gnn_b1': _L0_gnn_in['b1'], 'L0_gnn_W2': _L0_gnn_in['W2'], 'L0_gnn_b2': _L0_gnn_in['b2'], 'L1_gnn_deg_hist': _L1_gnn_in['deg_hist'], 'L1_gnn_W_e': _L1_gnn_in['W_e'], 'L1_gnn_b_e': _L1_gnn_in['b_e'], 'L1_gnn_W_pre': _L1_gnn_in['W_pre'], 'L1_gnn_b_pre': _L1_gnn_in['b_pre'], 'L1_gnn_W_post': _L1_gnn_in['W_post'], 'L1_gnn_b_post': _L1_gnn_in['b_post'], 'L1_gnn_W_lin': _L1_gnn_in['W_lin'], 'L1_gnn_b_lin': _L1_gnn_in['b_lin']}

def reference(x, src, dst, edge_attr_64, L0_gnn_W1, L0_gnn_b1, L0_gnn_W2, L0_gnn_b2, L1_gnn_deg_hist, L1_gnn_W_e, L1_gnn_b_e, L1_gnn_W_pre, L1_gnn_b_pre, L1_gnn_W_post, L1_gnn_b_post, L1_gnn_W_lin, L1_gnn_b_lin):
    import jax
    import jax.numpy as jnp

    def _L0_gnn_ref(v0, edge_index, W1, b1, W2, b2):
        import jax, jax.numpy as jnp
        import numpy as np
        N_NODES = 100000
        N_EDGES = 25000
        D = 64

        def _gcn_conv(x, src, dst, W, b, n_nodes):
            h = x @ W
            agg = jax.ops.segment_sum(h[src], dst, num_segments=n_nodes)
            return agg + b
        src = edge_index[0]
        dst = edge_index[1]
        n = v0.shape[0]
        x = _gcn_conv(v0, src, dst, W1, b1, n)
        x = jax.nn.relu(x)
        return _gcn_conv(x, src, dst, W2, b2, n)

    def _L1_gnn_ref(x, edge_attr, edge_index, deg_hist, W_e, b_e, W_pre, b_pre, W_post, b_post, W_lin, b_lin):
        import jax, jax.numpy as jnp
        import numpy as np
        N = 1024
        E = 16384
        F = 64
        NUM_AGGR = 4
        NUM_SCALER = 3
        EPS = 1e-05

        def _linear_init(key, fan_in, fan_out):
            kw, kb = jax.random.split(key)
            s = 1.0 / np.sqrt(fan_in)
            W = jax.random.uniform(kw, (fan_in, fan_out), jnp.float32, -s, s)
            b = jax.random.uniform(kb, (fan_out,), jnp.float32, -s, s)
            return (W, b)
        n = x.shape[0]
        src, dst = (edge_index[0], edge_index[1])
        dh = deg_hist.astype(jnp.float32)
        bins = jnp.arange(dh.shape[0], dtype=jnp.float32)
        avg_log = jnp.sum(jnp.log(bins + 1.0) * dh) / jnp.sum(dh)
        e = edge_attr @ W_e + b_e
        h = jnp.concatenate([x[dst], x[src], e], axis=-1)
        h = h @ W_pre + b_pre
        cnt = jax.ops.segment_sum(jnp.ones((h.shape[0],), h.dtype), dst, num_segments=n)
        deg = jnp.clip(cnt, 1.0)[:, None]
        s = jax.ops.segment_sum(h, dst, num_segments=n)
        mean = s / deg
        mean_sq = jax.ops.segment_sum(h * h, dst, num_segments=n) / deg
        var = mean_sq - mean * mean
        std = jnp.sqrt(jax.nn.relu(var) + EPS)
        has_edge = (cnt > 0)[:, None]
        mn = jnp.where(has_edge, jax.ops.segment_min(h, dst, num_segments=n), 0.0)
        mx = jnp.where(has_edge, jax.ops.segment_max(h, dst, num_segments=n), 0.0)
        agg = jnp.concatenate([mean, mn, mx, std], axis=-1)
        log_deg = jnp.log(deg + 1.0)
        out = jnp.concatenate([agg, agg * (log_deg / avg_log), agg * (avg_log / log_deg)], axis=-1)
        out = jnp.concatenate([x, out], axis=-1)
        out = out @ W_post + b_post
        out = out @ W_lin + b_lin
        return out
    edge_index = jnp.stack([src, dst])
    h = jnp.maximum(_layernorm(x, axis=-1), 0.0)
    x = x + _L0_gnn_ref(h, edge_index, L0_gnn_W1, L0_gnn_b1, L0_gnn_W2, L0_gnn_b2)
    h = jnp.maximum(_layernorm(x, axis=-1), 0.0)
    x = x + _L1_gnn_ref(h, edge_attr_64, edge_index, L1_gnn_deg_hist, L1_gnn_W_e, L1_gnn_b_e, L1_gnn_W_pre, L1_gnn_b_pre, L1_gnn_W_post, L1_gnn_b_post, L1_gnn_W_lin, L1_gnn_b_lin)
    return x

_drawn_inputs = setup_inputs


def setup_inputs(seed=0):
    import zlib

    import numpy as np

    out = dict(_drawn_inputs(seed))
    spreads = {'L0_gnn_b1': (0.0, 0.1), 'L0_gnn_b2': (0.0, 0.1)}
    factors = {'L1_gnn_b_e': 6.801, 'L1_gnn_b_pre': 3.591, 'L1_gnn_b_post': 4.597}
    for name, (base, spread) in spreads.items():
        noise = np.random.default_rng([zlib.crc32(name.encode()), seed]).standard_normal(out[name].shape)
        drawn = base * np.exp(spread * noise) if base else spread * noise
        out[name] = jnp.asarray(drawn.astype(out[name].dtype))
    for name, factor in factors.items():
        out[name] = (out[name] * factor).astype(out[name].dtype)
    return out
```

```python
import concourse.bass as bass
from concourse import mybir
from contextlib import ExitStack

F32, BF16, I32, U32 = mybir.dt.float32, mybir.dt.bfloat16, mybir.dt.int32, mybir.dt.uint32
ALU = mybir.AluOpType
ACT = mybir.ActivationFunctionType
AX = mybir.AxisListType.X

N, E, D, P = 100000, 50000, 64, 128
TILES = 4
GROUP = TILES * P
GROUPS = -(-E // GROUP)
PAIRS = GROUPS // 2
EP = GROUPS * GROUP
TAIL = (E - (GROUPS - 1) * GROUP) // TILES
DTAIL = (N - (2 * GROUPS - 1) * GROUP) // TILES
DEFAULT = EP
FAR = 1 << 20
LOW = -3.0e38
EPS = 1e-5
BINS = 32
assert GROUPS % 2 == 0 and 0 < DTAIL <= P and (E - (GROUPS - 1) * GROUP) % TILES == 0


def need(eng, sem, value):
    if not isinstance(value, int) or value > 0:
        eng.wait_ge(sem, value)


def settle(eng):
    eng.nop(nofuse=True)


class Order:

    def __init__(self, eng, sem, n):
        self.eng, self.sem, self.n = eng, sem, n

    def begin(self, turn):
        self.base, self.k = turn * self.n, 0

    def link(self, ins):
        ins.then_inc(self.sem, 1)
        self.k += 1
        self.eng.wait_ge(self.sem, self.base + self.k)

    def end(self):
        assert self.k == self.n, (self.k, self.n)


def turns(eng, step):
    step(0, 0)
    step(0, 1)
    step(1, 0)
    with eng.Fori(1, PAIRS - 1) as i:
        step(i, 1)
        step(i + 1, 0)
    step(PAIRS - 1, 1)


def before(i, s):
    if s == 1:
        return i, 0
    if isinstance(i, int) and i == 0:
        return None
    return i - 1, 1


def gnn(nc, x, src, dst, edge_attr, W1, b1, W2, b2, deg_hist, W_e, b_e, W_pre, b_pre,
        W_post, b_post, W_lin, b_lin, out):
    with ExitStack() as ctx:
        def sb(name, shape, dt=F32):
            return ctx.enter_context(nc.sbuf_tensor(name, shape, dt))

        def sem(name):
            return ctx.enter_context(nc.semaphore(name))

        def two(name):
            return [sem(f"{name}_{s}") for s in range(2)]

        slot_of = nc.dram_tensor("slot_of", (N, 1), I32).ap()
        hop1 = nc.dram_tensor("hop1", (EP + 1, D), F32).ap()
        hop2 = nc.dram_tensor("hop2", (EP + 1, D), F32).ap()
        xsrc_d = nc.dram_tensor("xsrc_d", (EP, D), F32).ap()
        slots_d = nc.dram_tensor("slots_d", (EP, 1), I32).ap()
        keep_d = nc.dram_tensor("keep_d", (1, EP), BF16).ap()
        low_d = nc.dram_tensor("low_d", (1, EP), BF16).ap()
        irec_d = nc.dram_tensor("irec_d", (EP, 3), I32).ap()
        frec_d = nc.dram_tensor("frec_d", (EP, 3), F32).ap()

        R = GROUPS
        dsti = sb("dsti", [R, GROUP], I32)
        nexti = sb("nexti", [R, GROUP], I32)
        previ = sb("previ", [R, GROUP], I32)
        keep = sb("keep", [R, GROUP])
        same_next = sb("same_next", [R, GROUP])
        keep_b = sb("keep_b", [R, GROUP], BF16)
        low_b = sb("low_b", [R, GROUP], BF16)
        ones = sb("ones", [P, GROUP])
        cnt = sb("cnt", [R, GROUP])
        whole = sb("whole", [R, GROUP])
        deg = sb("deg", [R, GROUP])
        logd = sb("logd", [R, GROUP])
        rlogd = sb("rlogd", [R, GROUP])
        irec_all = sb("irec_all", [R, GROUP, 3], I32)
        frec_all = sb("frec_all", [R, GROUP, 3])
        ends = sb("ends", [1, 2, P])
        carry = sb("carry", [1, R + 1])
        carry_col = sb("carry_col", [R, 1])
        fill = sb("fill", [80, N // 80], I32)
        ident = sb("ident", [P, P])
        eps_col = sb("eps_col", [P, 1])
        one_col = sb("one_col", [P, 1])
        sign = sb("sign", [P, 1])
        w1 = sb("w1", [D + 1, D])
        w2 = sb("w2", [D + 1, D])
        b1row = sb("b1row", [1, D])
        b1relu = sb("b1relu", [1, D])
        b2row = sb("b2row", [1, D])
        b2all = sb("b2all", [P, D])
        we = sb("we", [D, D])
        wedge = sb("wedge", [D, D])
        wcat = sb("wcat", [P, 2, D])
        wpd = sb("wpd", [D, D])
        wpdT = sb("wpdT", [D, D])
        weT = sb("weT", [D, P])
        be_col = sb("be_col", [D, 1])
        wpe2 = sb("wpe2", [D, 2, D])
        bpre2 = sb("bpre2", [P, 1])
        bias2 = sb("bias2", [P, 1])
        sbias2 = sb("sbias2", [P, 1])
        wlin = sb("wlin", [D, D])
        wpx = sb("wpx", [D, D])
        wpxT = sb("wpxT", [D, D])
        wps = sb("wps", [P, 6, D])
        wpsT = sb("wpsT", [D, 6, P])
        wsh = sb("wsh", [D, 3, 3, D])
        wsum = sb("wsum", [D, 3, D])
        wshT = sb("wshT", [D, 3, D])
        wshTx = sb("wshTx", [D, D])
        bpost_col = sb("bpost_col", [D, 1])
        blin_row = sb("blin_row", [1, D])
        brow = sb("brow", [1, 3, D])
        crow = sb("crow", [1, D])
        f_ms = sb("f_ms", [P, 3 * D])
        f_xn = sb("f_xn", [P, 3 * D])
        f_h = sb("f_h", [D + 1, 3 * D])
        w_dense = sb("w_dense", [D + 1, D])
        hist_i = sb("hist_i", [P, BINS], I32)
        hist = sb("hist", [P, BINS])
        bins = sb("bins", [P, BINS])
        logb = sb("logb", [P, BINS])
        hl = sb("hl", [P, BINS])
        avg = sb("avg", [P, 8])
        coef = sb("coef", [P, 3])
        two_col = sb("two_col", [P, 2])

        ps = ctx.enter_context(nc.psum_tensor("ps", [P, 8, 512], F32))

        s_init = sem("constants_set")
        s_ident0 = sem("identity_cleared")
        s_ident = sem("identity_set")
        s_ld = sem("setup_loaded")
        s_iota = sem("positions_set")
        s_dv = sem("setup_vector")
        s_pe = sem("setup_products")
        s_ac = sem("setup_scalar")
        s_rec = sem("records_stored")
        s_fill = sem("slots_filled")
        s_def = sem("defaults_stored")
        s_wrow = sem("weight_rows_moved")
        s_wready = sem("weights_ready")
        s_recready = sem("records_ready")
        s_fready = sem("degree_records_ready")

        L = []
        for layer in (1, 2):
            n = lambda t: f"{t}{layer}"
            b = {}
            b["isrc"] = [sb(n(f"isrc{s}_"), [P, TILES], I32) for s in range(2)]
            b["irec"] = [sb(n(f"irec{s}_"), [P, TILES, 3], I32) for s in range(2)]
            b["slots"] = [sb(n(f"slots{s}_"), [P, TILES], I32) for s in range(2)]
            b["keep"] = [sb(n(f"kp{s}_"), [D, GROUP], BF16) for s in range(2)]
            b["x8"] = [sb(n(f"x8{s}_"), [P, 2 * TILES, D]) for s in range(2)]
            b["xc"] = sb(n("xc"), [P, 2 * TILES, D])
            b["sq"] = sb(n("sq"), [P, 2 * TILES, D])
            b["h8"] = [sb(n(f"h8{s}_"), [P, 2 * TILES, D]) for s in range(2)]
            b["st"] = sb(n("st"), [P, 4, 2 * TILES])
            b["hT"] = [sb(n(f"hT{s}_"), [D, GROUP]) for s in range(2)]
            b["dT"] = [sb(n(f"dT{s}_"), [D + 1, GROUP]) for s in range(2)]
            b["S"] = [sb(n(f"S{s}_"), [D + 1, GROUP]) for s in range(2)]
            b["z"] = [sb(n(f"z{s}_"), [P, TILES, D]) for s in range(2)]
            b["o"] = [sb(n(f"o{s}_"), [P, TILES, D]) for s in range(2)]
            base = 4 * (layer - 1)
            b["pT"], b["pD"], b["pZ"], b["pO"] = (ps[:, base + q, :] for q in range(4))
            for t in ("idx_loaded", "keep_loaded", "dense_loaded", "rows_gathered", "slots_moved",
                      "rows_saved", "hop_stored", "dense_stored"):
                b[t] = two(n(t + "_l"))
            for t in ("rows_read", "sumsq_ready", "std_ready", "h_ready", "transposed", "hT_ready",
                      "dT_ready", "scanned", "hop_product", "dense_product", "hop_ready", "dense_ready",
                      "vector_order"):
                b[t] = sem(n(t + "_l"))
            L.append(b)

        c = {}
        c["slots"] = [sb(f"slots3{s}", [P, TILES], I32) for s in range(2)]
        c["irec"] = [sb(f"irec3{s}", [P, TILES, 3], I32) for s in range(2)]
        c["frec"] = [sb(f"frec3{s}", [P, TILES, 3]) for s in range(2)]
        c["keep"] = [sb(f"keep3{s}", [P, GROUP], BF16) for s in range(2)]
        c["low"] = [sb(f"low3{s}", [P, GROUP], BF16) for s in range(2)]
        c["x8"] = [sb(f"x83{s}", [P, 2 * TILES, D]) for s in range(2)]
        c["y8"] = [sb(f"y83{s}", [P, 2 * TILES, D]) for s in range(2)]
        c["x2"] = [sb(f"x23{s}", [P, 2 * TILES, D]) for s in range(2)]
        c["xc"] = sb("xc3", [P, 2 * TILES, D])
        c["sq"] = sb("sq3", [P, 2 * TILES, D])
        c["st"] = sb("st3", [P, 4, 2 * TILES])
        c["cat"] = [sb(f"cat3{s}", [P, TILES, 2 * D]) for s in range(2)]
        c["hd"] = [sb(f"hd3{s}", [P, TILES, D]) for s in range(2)]
        c["catT"] = sb("catT3", [P, GROUP])
        c["hdT"] = [sb(f"hdT3{s}", [D + 1, GROUP]) for s in range(2)]
        c["u1"] = sb("u13", [P, GROUP])
        c["u2"] = sb("u23", [P, GROUP])
        c["r1"] = [sb(f"r13{s}", [P, GROUP]) for s in range(2)]
        c["r2"] = [sb(f"r23{s}", [P, GROUP]) for s in range(2)]
        c["ms"] = sb("ms3", [P, TILES, 2 * D])
        c["m2"] = sb("m23", [P, TILES, D])
        c["var"] = sb("var3", [P, TILES, D])
        c["msT"] = sb("msT3", [P, GROUP])
        c["t1"] = sb("t13", [P, TILES, D])
        c["t2"] = sb("t23", [P, TILES, D])
        c["o1"] = sb("o13", [P, TILES, D])
        c["o"] = [sb(f"o3{s}", [P, TILES, D]) for s in range(2)]
        pCat, pC, pH, pR, pM = (ps[:, q, :] for q in range(5))
        pF = ps[:, 6:8, :].rearrange("p b (k n) -> p (b k) n", n=256)
        for t in ("idx_loaded", "frec_loaded", "masks_loaded", "x_loaded", "attr_loaded", "hop2_gathered", "x_gathered",
                  "out_stored"):
            c[t] = two(t + "_3")
        for t in ("summed", "rows_read", "sumsq_ready", "std_ready", "h_ready", "catT_done", "catT_ready", "msg_done", "hdT_done",
                  "hdT_ready", "msg_ready", "scanned", "back_done", "moments_read", "var_ready", "spread_ready",
                  "msT_done", "msT_ready", "final_done", "final_read", "out_ready", "order_a", "order_c", "order_d"):
            c[t] = sem(t + "_3")

        block = ctx.enter_context(nc.Block())

        def grp(ap, i, s, rows=P):
            if isinstance(i, int):
                r0 = (2 * i + s) * GROUP
                return ap[r0:r0 + rows * TILES].rearrange("(p k) f -> p (k f)", k=TILES)
            return ap[bass.ds(i * (2 * GROUP) + s * GROUP, rows * TILES)].rearrange("(p k) f -> p (k f)", k=TILES)

        def last(i, s):
            return isinstance(i, int) and i == PAIRS - 1 and s == 1

        def dense_rows(ap, layer, i, s):
            full = not (layer == 2 and last(i, s))
            rows = P if full else DTAIL
            off = (layer - 1) * GROUPS * GROUP
            if isinstance(i, int):
                r0 = off + (2 * i + s) * GROUP
                v = ap[r0:r0 + rows * TILES]
            else:
                v = ap[bass.ds(i * (2 * GROUP) + s * GROUP + off, rows * TILES)]
            return v.rearrange("(p k) f -> p (k f)", k=TILES), rows

        def mask(ap, i, s, parts):
            if isinstance(i, int):
                v = ap[:, (2 * i + s) * GROUP:(2 * i + s + 1) * GROUP]
            else:
                v = ap[:, bass.ds(i * (2 * GROUP) + s * GROUP, GROUP)]
            return v.to_broadcast([parts, GROUP])

        src2 = src.rearrange("(e o) -> e o", o=1)
        col = lambda v: v.rearrange("(p o) -> p o", o=1)
        row = lambda v: v.rearrange("(o f) -> o f", o=1)
        loads = []
        full = (R - 1) * GROUP
        flat = lambda v: v.rearrange("(r c) -> r c", c=GROUP)
        loads += [(dsti[0:R - 1, :], flat(dst[0:full])),
                  (dsti[R - 1:R, 0:E - full], row(dst[full:E])),
                  (nexti[0:R - 1, :], flat(dst[1:full + 1])),
                  (nexti[R - 1:R, 0:E - full - 1], row(dst[full + 1:E])),
                  (previ[0:1, 1:GROUP], row(dst[0:GROUP - 1])),
                  (previ[1:R - 1, :], flat(dst[GROUP - 1:full - 1])),
                  (previ[R - 1:R, 0:E - full + 1], row(dst[full - 1:E]))]
        wloads = [(w1[0:D, :], W1), (w1[D:D + 1, :], row(b1)), (w2[0:D, :], W2), (w2[D:D + 1, :], row(b2)),
                  (b1row[:, :], row(b1)), (b2row[:, :], row(b2)), (b2all[:, :], row(b2).to_broadcast([P, D])),
                  (we[:, :], W_e), (wedge[:, :], W_pre[2 * D:3 * D, :]), (be_col[:, :], col(b_e)),
                  (wcat[0:D, 0, :], W_pre[D:2 * D, :]), (wcat[0:D, 1, :], W_pre[D:2 * D, :]),
                  (wpd[:, :], W_pre[0:D, :]), (wpe2[:, 0, :], W_pre[2 * D:3 * D, :]),
                  (wpe2[:, 1, :], W_pre[2 * D:3 * D, :]), (bpre2[0:D, :], col(b_pre)), (bpre2[D:P, :], col(b_pre)),
                  (wlin[:, :], W_lin), (wpx[:, :], W_post[0:D, :]), (bpost_col[:, :], col(b_post)),
                  (blin_row[:, :], row(b_lin)), (hist_i[:, :], row(deg_hist).to_broadcast([P, BINS]))]
        MEAN, MIN, MAX, STD = range(4)
        post = lambda j, a: W_post[D + (j * 4 + a) * D:D + (j * 4 + a + 1) * D, :]
        for j in range(3):
            for q, (a0, a1) in enumerate(((MEAN, STD), (MAX, MIN))):
                wloads += [(wps[0:D, 3 * q + j, :], post(j, a0)), (wps[D:P, 3 * q + j, :], post(j, a1))]
            for a in (MEAN, MIN, MAX):
                wloads.append((wsh[:, j, a, :], post(j, a)))

        @block.sync
        def _(sp):
            sp.wait_ge(s_init, 3)
            with nc.allow_non_contiguous_dma(reason="columns of a bias"):
                for d, v in loads + wloads:
                    sp.dma_start(d, v).then_inc(s_ld, 16)
            sp.wait_ge(s_recready, 1)
            sp.wait_ge(s_iota, 1)
            sp.dma_start(keep_d.rearrange("o (r c) -> (o r) c", c=GROUP), keep_b[:, :]).then_inc(s_rec, 16)
            sp.dma_start(low_d.rearrange("o (r c) -> (o r) c", c=GROUP), low_b[:, :]).then_inc(s_rec, 16)
            sp.dma_start(irec_d.rearrange("(r c) f -> r (c f)", c=GROUP),
                         irec_all[:, :, :].rearrange("r c f -> r (c f)")).then_inc(s_rec, 16)
            sp.wait_ge(s_rec, 48)

            for layer in (1, 2):
                b = L[layer - 1]

                def step(i, s):
                    rows = TAIL if last(i, s) else P
                    if layer == 1:
                        need(sp, b["rows_gathered"][s], 64 * i)
                        need(sp, b["slots_moved"][s], 64 * i)
                        settle(sp)
                        sp.dma_start(b["irec"][s][:, :, :].rearrange("p k f -> p (k f)"),
                                     grp(irec_d, i, s)).then_inc(b["idx_loaded"][s], 16)
                    else:
                        need(sp, b["slots_moved"][s], 64 * i)
                        settle(sp)
                    sp.dma_start(b["isrc"][s][0:rows, :], grp(src2, i, s, rows)).then_inc(b["idx_loaded"][s], 16)
                    need(sp, b["dense_stored"][s], 16 * i)
                    settle(sp)
                    v, r = dense_rows(x, layer, i, s)
                    sp.dma_start(b["x8"][s][0:r, TILES:2 * TILES, :].rearrange("p k f -> p (k f)"),
                                 v).then_inc(b["dense_loaded"][s], 16)
                    need(sp, b["scanned"], (2 * i + s) - 1)
                    settle(sp)
                    sp.dma_start(b["keep"][s][:, :], mask(keep_d, i, s, D)).then_inc(b["keep_loaded"][s], 16)

                turns(sp, step)

            for s in range(2):
                sp.wait_ge(L[0]["rows_saved"][s], 16 * PAIRS)
                sp.wait_ge(L[1]["rows_saved"][s], 16 * PAIRS)
                sp.wait_ge(L[1]["hop_stored"][s], 16 * PAIRS)
            sp.wait_ge(s_fready, 1)
            sp.dma_start(frec_d.rearrange("(r c) f -> r (c f)", c=GROUP),
                         frec_all[:, :, :].rearrange("r c f -> r (c f)")).then_inc(s_rec, 16)
            sp.wait_ge(s_rec, 64)

            def step3(i, s):
                need(sp, c["out_stored"][s], 64 * i)
                settle(sp)
                sp.dma_start(c["irec"][s][:, :, :].rearrange("p k f -> p (k f)"),
                             grp(irec_d, i, s)).then_inc(c["idx_loaded"][s], 16)
                sp.dma_start(c["slots"][s][:, :], grp(slots_d, i, s)).then_inc(c["idx_loaded"][s], 16)
                need(sp, c["summed"], (2 * i + s) - 1)
                settle(sp)
                flat3 = lambda t: t.rearrange("p k f -> p (k f)")
                sp.dma_start(flat3(c["x8"][s][:, 0:TILES, :]), grp(xsrc_d, i, s)).then_inc(c["x_loaded"][s], 16)
                sp.dma_start(flat3(c["y8"][s][:, TILES:2 * TILES, :]), grp(hop2, i, s)).then_inc(c["x_loaded"][s], 16)
                need(sp, c["catT_done"], (2 * i + s) - 1)
                settle(sp)
                rows = TAIL if last(i, s) else P
                sp.dma_start(c["cat"][s][0:rows, :, D:2 * D],
                             grp(edge_attr, i, s, rows).rearrange("p (k f) -> p k f", f=D)).then_inc(
                                 c["attr_loaded"][s], 16)
                need(sp, c["scanned"], 2 * (2 * i + s) - 2)
                settle(sp)
                sp.dma_start(c["keep"][s][:, :], mask(keep_d, i, s, P)).then_inc(c["masks_loaded"][s], 16)
                sp.dma_start(c["low"][s][:, :], mask(low_d, i, s, P)).then_inc(c["masks_loaded"][s], 16)
                need(sp, c["out_ready"], (2 * i + s) - 1)
                settle(sp)
                sp.dma_start(c["frec"][s][:, :, :].rearrange("p k f -> p (k f)"),
                             grp(frec_d, i, s)).then_inc(c["frec_loaded"][s], 16)

            turns(sp, step3)
            for s in range(2):
                sp.wait_ge(c["out_stored"][s], 64 * PAIRS)

        @block.gpsimd
        def _(pool):
            pool.iota(irec_all[:, :, 2], pattern=[[1, GROUP]], base=0, channel_multiplier=GROUP).then_inc(s_iota, 1)
            pool.memset(ident[:, :], 0.0).then_inc(s_ident0, 1)
            pool.wait_ge(s_ident0, 1)
            pool.affine_select(out=ident[:, :], in_=ident[:, :], compare_op=ALU.not_equal, fill=1.0, base=0,
                               pattern=[[-1, P]], channel_multiplier=1).then_inc(s_ident, 1)
            pool.iota(bins[:, :], pattern=[[1, BINS]], base=1, channel_multiplier=0,
                      allow_small_or_imprecise_dtypes=True).then_inc(s_iota, 1)

            def gather(dest, table, index, done):
                pool.indirect_dma_start(dest, None, table, bass.IndirectOffsetOnAxis(ap=index.bitcast(U32), axis=0)
                                        ).then_inc(done, 16)

            def scatter(table, index, source, done):
                pool.indirect_dma_start(table, bass.IndirectOffsetOnAxis(ap=index.bitcast(U32), axis=0), source,
                                        None, bounds_check=N - 1, oob_is_err=False).then_inc(done, 16)

            pool.wait_ge(s_fill, 16)
            b = L[0]

            def step1(i, s):
                pool.wait_ge(b["idx_loaded"][s], 32 * i + 32)
                need(pool, b["rows_saved"][s], 16 * i)
                need(pool, b["rows_read"], (2 * i + s) - 1)
                settle(pool)
                for k in range(TILES):
                    gather(b["x8"][s][:, k, :], x, b["isrc"][s][:, k:k + 1], b["rows_gathered"][s])
                for k in range(TILES):
                    scatter(slot_of, b["irec"][s][:, k, 0:1], b["irec"][s][:, k, 2:3], b["slots_moved"][s])

            turns(pool, step1)

            q = L[1]
            for s in range(2):
                pool.wait_ge(b["slots_moved"][s], 64 * PAIRS)
                pool.wait_ge(b["hop_stored"][s], 16 * PAIRS)
            pool.wait_ge(s_def, 32)

            def rows2(i, s):
                pool.wait_ge(q["slots_moved"][s], 64 * i + 64)
                need(pool, q["transposed"], (2 * i + s) - 1)
                settle(pool)
                for k in range(TILES):
                    gather(q["x8"][s][:, k, :], hop1, q["slots"][s][:, k:k + 1], q["rows_gathered"][s])

            def step2(i, s):
                pool.wait_ge(q["idx_loaded"][s], 16 * i + 16)
                need(pool, q["rows_gathered"][s], 64 * i)
                need(pool, q["rows_saved"][s], 16 * i)
                settle(pool)
                for k in range(TILES):
                    gather(q["slots"][s][:, k:k + 1], slot_of, q["isrc"][s][:, k:k + 1], q["slots_moved"][s])
                if before(i, s):
                    rows2(*before(i, s))

            turns(pool, step2)
            rows2(PAIRS - 1, 1)

            for s in range(2):
                pool.wait_ge(q["hop_stored"][s], 16 * PAIRS)
                pool.wait_ge(L[0]["dense_stored"][s], 16 * PAIRS)
                pool.wait_ge(q["dense_stored"][s], 16 * PAIRS)

            def out3(i, s):
                pool.wait_ge(c["out_ready"], 2 * i + s + 1)
                settle(pool)
                for k in range(TILES):
                    scatter(out, c["irec"][s][:, k, 0:1], c["o"][s][:, k, :], c["out_stored"][s])

            def step3(i, s):
                pool.wait_ge(c["idx_loaded"][s], 32 * i + 32)
                need(pool, c["summed"], (2 * i + s) - 1)
                settle(pool)
                for k in range(TILES):
                    gather(c["y8"][s][:, k, :], hop2, c["slots"][s][:, k:k + 1], c["hop2_gathered"][s])
                for k in range(TILES):
                    gather(c["x8"][s][:, TILES + k, :], x, c["irec"][s][:, k, 1:2], c["x_gathered"][s])
                if before(i, s):
                    out3(*before(i, s))

            turns(pool, step3)
            out3(PAIRS - 1, 1)

        @block.tensor
        def _(pe):
            pe.wait_ge(s_ident, 1)
            nw = 16 * (len(loads) + len(wloads))
            pe.wait_ge(s_ld, nw)
            T = nc.tensor.transpose
            M = nc.tensor.matmul

            def mm(o, l, r, start=True, stop=True):
                return M(o, l, r, start=start, stop=stop)

            T(ps[0:D, 0, 0:D], we[:, :], ident[0:D, 0:D])
            T(ps[0:D, 0, D:2 * D], wpd[:, :], ident[0:D, 0:D])
            T(ps[0:D, 0, 2 * D:3 * D], wpx[:, :], ident[0:D, 0:D])
            for j in range(6):
                ins = T(ps[0:D, 1 + j // 3, (j % 3) * P:(j % 3 + 1) * P], wps[:, j, :], ident[:, :])
            ins.then_inc(s_pe, 1)
            pe.wait_ge(s_dv, 1)
            for j in range(3):
                mm(ps[0:D, 3, j * D:(j + 1) * D], wsum[:, j, :], wpdT[:, :])
            mm(ps[:, 4, 0:1], wpe2[:, :, :].rearrange("p a f -> p (a f)"), be_col[:, :])
            mm(ps[:, 4, 64:128], weT[:, :], wedge[:, :])
            for j in range(3):
                mm(ps[:, 5, j * D:(j + 1) * D], wpsT[:, j, :], wlin[:, :])
            for j in range(3):
                mm(ps[:, 6, j * D:(j + 1) * D], wpsT[:, 3 + j, :], wlin[:, :])
            mm(ps[0:1, 7, 0:D], bpost_col[:, :], wlin[:, :]).then_inc(s_pe, 1)
            pe.wait_ge(s_dv, 2)
            mm(ps[0:D, 0, 0:D], wshTx[:, :], wlin[:, :])
            for j in range(1, 3):
                mm(ps[0:D, 0, j * D:(j + 1) * D], wshT[:, j, :], wlin[:, :])
            mm(ps[0:D, 1, 0:D], wpxT[:, :], wlin[:, :])
            for j in range(3):
                ins = mm(ps[0:1, 2, 0:D], coef[:, j:j + 1], f_ms[:, j * D:(j + 1) * D], start=j == 0, stop=j == 2)
            ins.then_inc(s_pe, 1)
            pe.wait_ge(s_dv, 3)
            T(ps[0:1, 3, 0:R], cnt[:, GROUP - 1:GROUP], ident[0:R, 0:R])
            T(ps[0:1, 4, 0:R], whole[:, GROUP - 1:GROUP], ident[0:R, 0:R]).then_inc(s_pe, 1)
            pe.wait_ge(s_dv, 4)
            T(ps[0:R, 5, 0:1], carry[0:1, 0:R], ident[0:1, 0:1]).then_inc(s_pe, 1)
            pe.wait_ge(s_dv, 5)
            pe.wait_ge(s_wrow, 32)

            for layer in (1, 2):
                b = L[layer - 1]
                w = (w1, w2)[layer - 1]

                def products(i, s):
                    g = 2 * i + s
                    pe.wait_ge(b["dT_ready"], g + 1)
                    need(pe, b["dense_ready"], g)
                    for k in range(TILES):
                        ins = mm(b["pO"][:, k * D:(k + 1) * D], b["dT"][s][:, k * P:(k + 1) * P], w_dense[:, :])
                    ins.then_inc(b["dense_product"], 1)
                    pe.wait_ge(b["scanned"], g + 1)
                    need(pe, b["hop_ready"], g)
                    for k in range(TILES):
                        ins = mm(b["pZ"][:, k * D:(k + 1) * D], b["S"][s][:, k:GROUP:TILES], w[:, :])
                    ins.then_inc(b["hop_product"], 1)

                def step(i, s):
                    g = 2 * i + s
                    pe.wait_ge(b["h_ready"], g + 1)
                    if layer == 2:
                        pe.wait_ge(b["rows_gathered"][s], 64 * i + 64)
                    need(pe, b["dT_ready"], g)
                    settle(pe)
                    for k in range(TILES):
                        T(b["pD"][0:D, k * P:(k + 1) * P], b["h8"][s][:, TILES + k, :], ident[:, :])
                    rows = b["h8"] if layer == 1 else b["x8"]
                    for k in range(TILES):
                        ins = T(b["pT"][0:D, k:GROUP:TILES], rows[s][:, k, :], ident[:, :])
                    ins.then_inc(b["transposed"], 1)
                    if before(i, s):
                        products(*before(i, s))

                turns(pe, step)
                products(PAIRS - 1, 1)

            for s in range(2):
                pe.wait_ge(L[1]["hop_stored"][s], 16 * PAIRS)
                pe.wait_ge(L[1]["dense_stored"][s], 16 * PAIRS)

            def finals(i, s):
                g = 2 * i + s
                pe.wait_ge(c["spread_ready"], g + 1)
                need(pe, c["msT_ready"], g)
                for k in range(TILES):
                    ins = T(pM[:, k * P:(k + 1) * P], c["ms"][:, k, :], ident[:, :])
                ins.then_inc(c["msT_done"], 1)
                pe.wait_ge(c["msT_ready"], g + 1)
                pe.wait_ge(c["hdT_ready"], g + 1)
                need(pe, c["final_read"], g)
                for k in range(TILES):
                    mm(pF[:, k, 0:3 * D], c["r2"][s][:, k:GROUP:TILES], f_xn[:, :], stop=False)
                    mm(pF[:, k, 0:3 * D], c["hdT"][s][:, k * P:(k + 1) * P], f_h[:, :], start=False, stop=False)
                    ins = mm(pF[:, k, 0:3 * D], c["msT"][:, k * P:(k + 1) * P], f_ms[:, :], start=False)
                ins.then_inc(c["final_done"], 1)

            def step3(i, s):
                g = 2 * i + s
                pe.wait_ge(c["h_ready"], g + 1)
                pe.wait_ge(c["attr_loaded"][s], 16 * i + 16)
                need(pe, c["catT_ready"], g)
                for k in range(TILES):
                    ins = T(pCat[:, k:GROUP:TILES], c["cat"][s][:, k, :], ident[:, :])
                ins.then_inc(c["catT_done"], 1)
                need(pe, c["hdT_ready"], g)
                settle(pe)
                for k in range(TILES):
                    ins = T(pH[0:D, k * P:(k + 1) * P], c["hd"][s][:, k, :], ident[:, :])
                ins.then_inc(c["hdT_done"], 1)
                pe.wait_ge(c["catT_ready"], g + 1)
                need(pe, c["msg_ready"], g)
                mm(pC[:, :], wcat[:, :, :].rearrange("p a f -> p (a f)"), c["catT"][:, :]).then_inc(c["msg_done"], 1)
                if before(i, s):
                    finals(*before(i, s))
                pe.wait_ge(c["scanned"], 2 * g + 2)
                need(pe, c["moments_read"], g)
                for k in range(TILES):
                    ins = T(pR[:, k * P:(k + 1) * P], c["r1"][s][:, k:GROUP:TILES], ident[:, :])
                ins.then_inc(c["back_done"], 1)

            turns(pe, step3)
            finals(PAIRS - 1, 1)

        @block.scalar
        def _(act):
            A = nc.scalar.activation
            act.wait_ge(s_init, 4)
            act.dma_start(slot_of.rearrange("(p c) o -> p (c o)", p=80), fill[:, :]).then_inc(s_fill, 16)
            act.wait_ge(s_iota, 2)
            A(logb[:, :], bins[:, :], ACT.Ln).then_inc(s_ac, 1)
            A(two_col[:, 0:1], one_col[:, :], ACT.Ln, bias=one_col[:, :]).then_inc(s_ac, 1)
            A(two_col[:, 1:2], one_col[:, :], ACT.Sqrt, bias=eps_col[:, :], scale=0.0).then_inc(s_ac, 1)
            act.wait_ge(s_dv, 2)
            act.dma_start(hop1[DEFAULT:DEFAULT + 1, :], b1relu[:, :]).then_inc(s_def, 16)
            act.dma_start(hop2[DEFAULT:DEFAULT + 1, :], b2row[:, :]).then_inc(s_def, 16)
            act.dma_start(f_h[D:D + 1, :], brow[:, :, :].rearrange("o a f -> o (a f)")).then_inc(s_wrow, 16)
            act.wait_ge(s_dv, 5)
            act.dma_start(w_dense[D:D + 1, :], crow[:, :]).then_inc(s_wrow, 16)
            act.wait_ge(s_dv, 6)
            A(logd[:, :], deg[:, :], ACT.Ln, bias=one_col[0:R, :]).then_inc(s_ac, 1)

            flat3 = lambda t: t.rearrange("p k f -> p (k f)")
            for layer in (1, 2):
                b = L[layer - 1]

                def stores(i, s):
                    g = 2 * i + s
                    act.wait_ge(b["hop_product"], g + 1)
                    need(act, b["hop_stored"][s], 16 * i)
                    A(flat3(b["z"][s][:, :, :]), b["pZ"][:, 0:TILES * D],
                      ACT.Relu if layer == 1 else ACT.Copy).then_inc(b["hop_ready"], 1)
                    act.wait_ge(b["hop_ready"], g + 1)
                    act.dma_start(grp((hop1, hop2)[layer - 1], i, s), flat3(b["z"][s][:, :, :])).then_inc(
                        b["hop_stored"][s], 16)
                    act.wait_ge(b["dense_ready"], g + 1)
                    v, r = dense_rows(out, layer, i, s)
                    act.dma_start(v, flat3(b["o"][s][0:r, :, :])).then_inc(b["dense_stored"][s], 16)

                def step(i, s):
                    g = 2 * i + s
                    lo = 0 if layer == 1 else TILES
                    if layer == 1:
                        act.wait_ge(b["rows_gathered"][s], 64 * i + 64)
                        act.dma_start(grp(xsrc_d, i, s), flat3(b["x8"][s][:, 0:TILES, :])).then_inc(
                            b["rows_saved"][s], 16)
                    else:
                        act.wait_ge(b["slots_moved"][s], 64 * i + 64)
                        act.dma_start(grp(slots_d, i, s), b["slots"][s][:, :]).then_inc(b["rows_saved"][s], 16)
                    act.wait_ge(b["sumsq_ready"], g + 1)
                    A(b["st"][:, 2, lo:], b["st"][:, 1, lo:], ACT.Sqrt, bias=eps_col[:, :],
                      scale=1.0 / D).then_inc(b["std_ready"], 1)
                    act.wait_ge(b["transposed"], g + 1)
                    need(act, b["scanned"], g - 1)
                    A(b["hT"][s][:, :], b["pT"][0:D, :], ACT.Copy).then_inc(b["hT_ready"], 1)
                    need(act, b["dense_product"], g - 1)
                    A(b["dT"][s][0:D, :], b["pD"][0:D, :], ACT.Copy).then_inc(b["dT_ready"], 1)
                    if before(i, s):
                        stores(*before(i, s))

                turns(act, step)
                stores(PAIRS - 1, 1)

            def spread(i, s):
                g = 2 * i + s
                act.wait_ge(c["var_ready"], g + 1)
                A(c["ms"][:, :, D:2 * D], c["var"][:, :, :], ACT.Sqrt).then_inc(c["spread_ready"], 1)
                act.wait_ge(c["msT_done"], g + 1)
                need(act, c["final_done"], g)
                A(c["msT"][:, :], pM[:, :], ACT.Copy).then_inc(c["msT_ready"], 1)

            def step3(i, s):
                g = 2 * i + s
                act.wait_ge(c["sumsq_ready"], g + 1)
                A(c["st"][:, 2, :], c["st"][:, 1, :], ACT.Sqrt, bias=eps_col[:, :], scale=1.0 / D).then_inc(
                    c["std_ready"], 1)
                act.wait_ge(c["catT_done"], g + 1)
                need(act, c["msg_done"], g)
                A(c["catT"][:, :], pCat[:, :], ACT.Copy).then_inc(c["catT_ready"], 1)
                act.wait_ge(c["hdT_done"], g + 1)
                need(act, c["final_done"], g - 1)
                A(c["hdT"][s][0:D, :], pH[0:D, :], ACT.Copy).then_inc(c["hdT_ready"], 1)
                act.wait_ge(c["msg_done"], g + 1)
                need(act, c["scanned"], 2 * g)
                A(c["u1"][0:D, :], pC[0:D, :], ACT.Identity, bias=bias2[0:D, :])
                A(c["u1"][D:P, :], pC[D:P, :], ACT.Square, bias=bias2[D:P, :])
                A(c["u2"][:, :], pC[:, :], ACT.Identity, bias=sbias2[:, :], scale=sign[:, :]).then_inc(
                    c["msg_ready"], 1)
                if before(i, s):
                    spread(*before(i, s))

            turns(act, step3)
            spread(PAIRS - 1, 1)

        @block.vector
        def _(dve):
            V = nc.vector
            V.memset(dsti[:, :], FAR).then_inc(s_init, 1)
            V.memset(nexti[:, :], FAR).then_inc(s_init, 1)
            V.memset(previ[:, :], -1).then_inc(s_init, 1)
            V.memset(one_col[:, :], 1.0)
            V.memset(eps_col[:, :], EPS)
            V.memset(fill[:, :], DEFAULT).then_inc(s_init, 1)
            V.memset(ones[:, :], 1.0)
            V.memset(sign[0:D, :], 1.0)
            V.memset(sign[D:P, :], -1.0)
            V.memset(weT[:, 0:D], 0.0)
            V.memset(coef[:, :], 0.0)
            V.memset(brow[:, :, :], 0.0)
            for t in (L[0]["isrc"], L[1]["isrc"]):
                for s in range(2):
                    V.memset(t[s][:, :], 0)
            for b in L:
                for s in range(2):
                    V.memset(b["dT"][s][D:D + 1, :], 1.0)
                    V.memset(b["S"][s][D:D + 1, :], 1.0)
            for s in range(2):
                V.memset(c["hdT"][s][D:D + 1, :], 1.0)
            chain = Order(dve, s_wready, 0)
            chain.begin(0)
            link = chain.link
            link(V.memset(carry[:, :], 0.0))
            nw = 16 * (len(loads) + len(wloads))
            dve.wait_ge(s_ld, nw)
            dve.wait_ge(s_pe, 1)
            V.tensor_copy(weT[:, D:P], ps[0:D, 0, 0:D])
            V.tensor_copy(wpdT[:, :], ps[0:D, 0, D:2 * D])
            V.tensor_copy(wpxT[:, :], ps[0:D, 0, 2 * D:3 * D])
            V.tensor_copy(wpsT[:, 0:3, :].rearrange("p a f -> p (a f)"), ps[0:D, 1, 0:3 * P])
            V.tensor_copy(wpsT[:, 3:6, :].rearrange("p a f -> p (a f)"), ps[0:D, 2, 0:3 * P])
            link(V.tensor_tensor(wsum[:, :, :], wsh[:, :, MEAN, :], wsh[:, :, MIN, :], ALU.add))
            V.tensor_tensor(wsum[:, :, :], wsum[:, :, :], wsh[:, :, MAX, :], ALU.add).then_inc(s_dv, 1)
            dve.wait_ge(s_ac, 3)
            link(V.tensor_copy(hist[:, :], hist_i[:, :]))
            link(V.tensor_tensor(hl[:, :], hist[:, :], logb[:, :], ALU.mult))
            link(V.tensor_reduce(avg[:, 0:1], hl[:, :], AX, ALU.add))
            link(V.tensor_reduce(avg[:, 1:2], hist[:, :], AX, ALU.add))
            link(V.reciprocal(avg[:, 2:3], avg[:, 1:2]))
            link(V.tensor_tensor(avg[:, 3:4], avg[:, 0:1], avg[:, 2:3], ALU.mult))
            link(V.reciprocal(avg[:, 4:5], avg[:, 3:4]))
            link(V.reciprocal(avg[:, 5:6], two_col[:, 0:1]))
            link(V.tensor_copy(coef[D:P, 0:1], two_col[D:P, 1:2]))
            link(V.tensor_tensor(avg[:, 6:7], two_col[:, 0:1], avg[:, 4:5], ALU.mult))
            link(V.tensor_tensor(avg[:, 7:8], avg[:, 3:4], avg[:, 5:6], ALU.mult))
            link(V.tensor_tensor(coef[D:P, 1:2], avg[D:P, 6:7], two_col[D:P, 1:2], ALU.mult))
            link(V.tensor_tensor(coef[D:P, 2:3], avg[D:P, 7:8], two_col[D:P, 1:2], ALU.mult))
            dve.wait_ge(s_pe, 2)
            V.tensor_copy(wshT[:, :, :].rearrange("p a f -> p (a f)"), ps[0:D, 3, 0:3 * D])
            V.tensor_tensor(wshTx[:, :], ps[0:D, 3, 0:D], wpxT[:, :], ALU.add)
            link(V.tensor_tensor(bias2[:, :], ps[:, 4, 0:1], bpre2[:, :], ALU.add))
            V.tensor_tensor(sbias2[:, :], bias2[:, :], sign[:, :], ALU.mult)
            for a in range(2):
                V.tensor_copy(wcat[D:P, a, :], ps[D:P, 4, D:2 * D])
            V.tensor_copy(f_ms[:, :], ps[:, 5, 0:3 * D])
            V.tensor_scalar(f_xn[:, :], ps[:, 6, 0:3 * D], sign[:, :], None, ALU.mult)
            V.tensor_scalar(b1relu[:, :], b1row[:, :], 0.0, None, ALU.max)
            V.tensor_tensor(brow[:, 0, :], ps[0:1, 7, 0:D], blin_row[:, :], ALU.add).then_inc(s_dv, 1)
            link(V.tensor_tensor(keep[:, :], dsti[:, :], previ[:, :], ALU.is_equal))
            link(V.tensor_tensor(same_next[:, :], dsti[:, :], nexti[:, :], ALU.is_equal))
            V.tensor_copy(keep_b[:, :], keep[:, :])
            V.tensor_scalar(low_b[:, :], keep[:, :], -1.0, -LOW, ALU.add, ALU.mult)
            V.tensor_scalar(irec_all[:, :, 1], dsti[:, :], float(N - 1), None, ALU.min)
            V.scalar_tensor_tensor(irec_all[:, :, 0], same_next[:, :], float(FAR), dsti[:, :], ALU.mult,
                                   ALU.add).then_inc(s_recready, 1)
            V.tensor_tensor_scan(cnt[:, :], keep[:, :], ones[0:R, :], 0.0, ALU.mult, ALU.add)
            V.tensor_tensor_scan(whole[:, :], keep[:, :], keep[:, :], 1.0, ALU.mult, ALU.mult).then_inc(s_dv, 1)
            dve.wait_ge(s_pe, 4)
            V.tensor_copy(ends[:, 0, 0:R], ps[0:1, 3, 0:R])
            link(V.tensor_copy(ends[:, 1, 0:R], ps[0:1, 4, 0:R]))
            V.tensor_tensor_scan(carry[:, 1:R + 1], ends[:, 1, 0:R], ends[:, 0, 0:R], 0.0, ALU.mult,
                                 ALU.add).then_inc(s_dv, 1)
            V.tensor_copy(f_h[0:D, :], ps[0:D, 0, 0:3 * D])
            V.tensor_copy(w_dense[0:D, :], ps[0:D, 1, 0:D])
            V.tensor_tensor(crow[:, :], ps[0:1, 2, 0:D], brow[:, 0, :], ALU.add).then_inc(s_dv, 1)
            dve.wait_ge(s_pe, 5)
            link(V.tensor_copy(carry_col[:, :], ps[0:R, 5, 0:1]))
            link(V.scalar_tensor_tensor(deg[:, :], whole[:, :], carry_col[:, :], cnt[:, :], ALU.mult, ALU.add))
            V.reciprocal(frec_all[:, :, 0], deg[:, :]).then_inc(s_dv, 1)
            dve.wait_ge(s_ac, 4)
            link(V.reciprocal(rlogd[:, :], logd[:, :]))
            V.tensor_scalar(frec_all[:, :, 1], logd[:, :], avg[0:R, 4:5], None, ALU.mult)
            V.tensor_scalar(frec_all[:, :, 2], rlogd[:, :], avg[0:R, 3:4], None, ALU.mult).then_inc(s_fready, 1)

            def wide(t, n):
                return t.rearrange("p (k o) -> p k o", o=1).to_broadcast([P, n, D])

            def moments(o, b, rows, lo, n, g, read, sumsq, std):
                hi = lo + n
                o.link(V.tensor_reduce(b["st"][:, 0, lo:hi], rows, AX, ALU.add))
                o.link(V.tensor_scalar(b["st"][:, 3, lo:hi], b["st"][:, 0, lo:hi], -1.0 / D, None, ALU.mult))
                ins = V.tensor_tensor(b["xc"][:, lo:hi, :], rows, wide(b["st"][:, 3, lo:hi], n), ALU.add)
                ins.then_inc(read, 1)
                dve.wait_ge(read, g + 1)
                o.link(V.tensor_tensor(b["sq"][:, lo:hi, :], b["xc"][:, lo:hi, :], b["xc"][:, lo:hi, :], ALU.mult))
                V.tensor_reduce(b["st"][:, 1, lo:hi], b["sq"][:, lo:hi, :], AX, ALU.add).then_inc(sumsq, 1)
                dve.wait_ge(std, g + 1)
                o.link(V.reciprocal(b["st"][:, 3, lo:hi], b["st"][:, 2, lo:hi]))

            for layer in (1, 2):
                b = L[layer - 1]
                o = Order(dve, b["vector_order"], 5)
                lo, n = (0, 2 * TILES) if layer == 1 else (TILES, TILES)

                def results(i, s):
                    g = 2 * i + s
                    dve.wait_ge(b["hT_ready"], g + 1)
                    dve.wait_ge(b["keep_loaded"][s], 16 * i + 16)
                    need(dve, b["scanned"], g)
                    need(dve, b["hop_product"], g - 1)
                    state = b["S"][1 - s][0:D, GROUP - 1:GROUP] if before(i, s) else 0.0
                    V.tensor_tensor_scan(b["S"][s][0:D, :], b["keep"][s][:, :], b["hT"][s][:, :], state,
                                         ALU.mult, ALU.add).then_inc(b["scanned"], 1)
                    dve.wait_ge(b["dense_product"], g + 1)
                    need(dve, b["dense_stored"][s], 16 * i)
                    V.tensor_tensor(b["o"][s][:, :, :],
                                    b["pO"][:, 0:TILES * D].rearrange("p (k f) -> p k f", f=D),
                                    b["x8"][s][:, TILES:2 * TILES, :], ALU.add).then_inc(b["dense_ready"], 1)

                def step(i, s):
                    g = 2 * i + s
                    o.begin(g)
                    dve.wait_ge(b["dense_loaded"][s], 16 * i + 16)
                    dx = b["x8"][s][:, TILES:2 * TILES, :]
                    bb = b2all[:, :].rearrange("p (o f) -> p o f", o=1).to_broadcast([P, TILES, D])
                    o.link(V.tensor_tensor(dx, dx, bb, ALU.add))
                    if layer == 1:
                        dve.wait_ge(b["rows_gathered"][s], 64 * i + 64)
                    moments(o, b, b["x8"][s][:, lo:lo + n, :], lo, n, g, b["rows_read"], b["sumsq_ready"],
                            b["std_ready"])
                    need(dve, b["transposed"], g - 1)
                    V.scalar_tensor_tensor(b["h8"][s][:, lo:lo + n, :], b["xc"][:, lo:lo + n, :], 0.0,
                                           wide(b["st"][:, 3, lo:lo + n], n), ALU.max, ALU.mult).then_inc(
                                               b["h_ready"], 1)
                    o.end()
                    if before(i, s):
                        results(*before(i, s))

                turns(dve, step)
                results(PAIRS - 1, 1)

            oa, oc, od = (Order(dve, c[t], k) for t, k in (("order_a", 4), ("order_c", 2), ("order_d", 1)))
            deg_of = lambda s, q: c["frec"][s][:, :, q:q + 1]

            def spread(i, s):
                g = 2 * i + s
                oc.begin(g)
                dve.wait_ge(c["back_done"], g + 1)
                dve.wait_ge(c["frec_loaded"][s], 16 * i + 16)
                need(dve, c["msT_done"], g)
                ins = V.tensor_tensor(c["ms"][:, :, :], pR[:, :].rearrange("p (k f) -> p k f", f=2 * D),
                                      deg_of(s, 0).to_broadcast([P, TILES, 2 * D]), ALU.mult)
                ins.then_inc(c["moments_read"], 1)
                dve.wait_ge(c["moments_read"], g + 1)
                oc.link(V.tensor_tensor(c["m2"][:, :, :], c["ms"][:, :, 0:D], c["ms"][:, :, 0:D], ALU.mult))
                need(dve, c["spread_ready"], g)
                oc.link(V.tensor_tensor(c["m2"][:, :, :], c["ms"][:, :, D:2 * D], c["m2"][:, :, :], ALU.subtract))
                V.tensor_scalar(c["var"][:, :, :], c["m2"][:, :, :], 0.0, EPS, ALU.max, ALU.add).then_inc(
                    c["var_ready"], 1)
                oc.end()

            def scans(i, s):
                g = 2 * i + s
                dve.wait_ge(c["msg_ready"], g + 1)
                dve.wait_ge(c["masks_loaded"][s], 32 * i + 32)
                need(dve, c["scanned"], 2 * g)
                need(dve, c["back_done"], g - 1)
                need(dve, c["final_done"], g - 1)
                first = before(i, s) is None
                V.tensor_tensor_scan(c["r1"][s][:, :], c["keep"][s][:, :], c["u1"][:, :],
                                     0.0 if first else c["r1"][1 - s][:, GROUP - 1:GROUP],
                                     ALU.mult, ALU.add).then_inc(c["scanned"], 1)
                V.tensor_tensor_scan(c["r2"][s][:, :], c["low"][s][:, :], c["u2"][:, :],
                                     LOW if first else c["r2"][1 - s][:, GROUP - 1:GROUP],
                                     ALU.add, ALU.max).then_inc(c["scanned"], 1)

            def final(i, s):
                g = 2 * i + s
                od.begin(g)
                dve.wait_ge(c["final_done"], g + 1)
                need(dve, c["out_stored"][s], 64 * i)
                V.tensor_tensor(c["o1"][:, :, :], pF[:, :, 0:D], c["x2"][s][:, TILES:2 * TILES, :], ALU.add)
                V.tensor_tensor(c["t1"][:, :, :], pF[:, :, D:2 * D], deg_of(s, 1).to_broadcast([P, TILES, D]),
                                ALU.mult)
                ins = V.tensor_tensor(c["t2"][:, :, :], pF[:, :, 2 * D:3 * D],
                                      deg_of(s, 2).to_broadcast([P, TILES, D]), ALU.mult)
                ins.then_inc(c["final_read"], 1)
                dve.wait_ge(c["final_read"], g + 1)
                od.link(V.tensor_tensor(c["t1"][:, :, :], c["t1"][:, :, :], c["t2"][:, :, :], ALU.add))
                V.tensor_tensor(c["o"][s][:, :, :], c["o1"][:, :, :], c["t1"][:, :, :], ALU.add).then_inc(
                    c["out_ready"], 1)
                od.end()

            def step3(i, s):
                g = 2 * i + s
                oa.begin(g)
                dve.wait_ge(c["x_loaded"][s], 32 * i + 32)
                dve.wait_ge(c["hop2_gathered"][s], 64 * i + 64)
                dve.wait_ge(c["x_gathered"][s], 64 * i + 64)
                need(dve, c["out_ready"], g - 1)
                V.tensor_tensor(c["x2"][s][:, :, :], c["x8"][s][:, :, :], c["y8"][s][:, :, :], ALU.add).then_inc(
                    c["summed"], 1)
                dve.wait_ge(c["summed"], g + 1)
                moments(oa, c, c["x2"][s][:, :, :], 0, 2 * TILES, g, c["rows_read"], c["sumsq_ready"],
                        c["std_ready"])
                need(dve, c["hdT_done"], g - 1)
                V.scalar_tensor_tensor(c["cat"][s][:, :, 0:D], c["xc"][:, 0:TILES, :], 0.0,
                                       wide(c["st"][:, 3, 0:TILES], TILES), ALU.max, ALU.mult)
                V.scalar_tensor_tensor(c["hd"][s][:, :, :], c["xc"][:, TILES:, :], 0.0,
                                       wide(c["st"][:, 3, TILES:], TILES), ALU.max, ALU.mult).then_inc(c["h_ready"], 1)
                oa.end()
                if before(i, s):
                    spread(*before(i, s))
                scans(i, s)
                if before(i, s):
                    final(*before(i, s))

            turns(dve, step3)
            spread(PAIRS - 1, 1)
            final(PAIRS - 1, 1)


_INS = ['x', 'src', 'dst', 'edge_attr_64', 'L0_gnn_W1', 'L0_gnn_b1', 'L0_gnn_W2', 'L0_gnn_b2', 'L1_gnn_deg_hist',
        'L1_gnn_W_e', 'L1_gnn_b_e', 'L1_gnn_W_pre', 'L1_gnn_b_pre', 'L1_gnn_W_post', 'L1_gnn_b_post',
        'L1_gnn_W_lin', 'L1_gnn_b_lin']


def kernel(**inputs):
    import numpy as _np
    import concourse.bacc as _bacc
    from concourse import mybir as _mybir
    from concourse.bass_utils import run_bass_kernel_spmd as _run

    nc = _bacc.Bacc("TRN2", target_bir_lowering=False, num_devices=1)
    arrays, args = {}, []
    for name in _INS:
        a = _np.ascontiguousarray(inputs[name])
        arrays[f"in_{name}_dram"] = a
        args.append(nc.dram_tensor(f"in_{name}_dram", a.shape, _mybir.dt.from_np(a.dtype), kind="ExternalInput").ap())
    args.append(nc.dram_tensor("out_0_dram", (N, D), _mybir.dt.float32, kind="ExternalOutput").ap())
    gnn(nc, *args)
    r = _run(nc, [arrays], core_ids=[0])
    return r.results[0]["out_0_dram"]
```

```python
import concourse.bass as bass
from concourse import mybir
from contextlib import ExitStack

F32, BF16, I32, U32 = mybir.dt.float32, mybir.dt.bfloat16, mybir.dt.int32, mybir.dt.uint32
ALU = mybir.AluOpType
ACT = mybir.ActivationFunctionType
AX = mybir.AxisListType.X

N, E, D, P = 100000, 50000, 64, 128
TILES = 4
GROUP = TILES * P
GROUPS = -(-E // GROUP)
SLOTS = 4
LAST = divmod(GROUPS - 1, SLOTS)
SCAN, SPREAD, FINISH, SCATTER = 1, 2, 3, 5
EP = GROUPS * GROUP
TAIL = (E - (GROUPS - 1) * GROUP) // TILES
DTAIL = (N - (2 * GROUPS - 1) * GROUP) // TILES
DEFAULT = EP
FAR = 1 << 20
LOW = -3.0e38
EPS = 1e-5
BINS = 32
assert GROUPS % SLOTS == 2 and 0 < DTAIL <= P and (E - (GROUPS - 1) * GROUP) % TILES == 0


def need(eng, sem, value):
    if not isinstance(value, int) or value > 0:
        eng.wait_ge(sem, value)


def settle(eng):
    eng.nop(nofuse=True)


class Order:

    def __init__(self, eng, sem, n):
        self.eng, self.sem, self.n = eng, sem, n

    def begin(self, turn):
        self.base, self.k = turn * self.n, 0

    def link(self, ins):
        ins.then_inc(self.sem, 1)
        self.k += 1
        self.eng.wait_ge(self.sem, self.base + self.k)

    def end(self):
        assert self.k == self.n, (self.k, self.n)


def turns(eng, step, first=SLOTS + 1):
    for g in range(first):
        step(*divmod(g, SLOTS))
    start, at = divmod(first, SLOTS)
    with eng.Fori(start, start + (GROUPS - first) // SLOTS) as i:
        for s in range(at, at + SLOTS):
            step(i + s // SLOTS if s >= SLOTS else i, s % SLOTS)
    for g in range(GROUPS - (GROUPS - first) % SLOTS, GROUPS):
        step(*divmod(g, SLOTS))


def before(i, s, n=1):
    back = -((s - n) // SLOTS)
    if isinstance(i, int) and i < back:
        return None
    return (i - back if back else i), (s - n) % SLOTS


def after_last(stage, lag):
    for g in range(GROUPS - lag, GROUPS):
        stage(*divmod(g, SLOTS))


def uses(s):
    return len(range(s, GROUPS, SLOTS))


def gnn(nc, x, src, dst, edge_attr, W1, b1, W2, b2, deg_hist, W_e, b_e, W_pre, b_pre,
        W_post, b_post, W_lin, b_lin, out):
    with ExitStack() as ctx:
        def sb(name, shape, dt=F32):
            return ctx.enter_context(nc.sbuf_tensor(name, shape, dt))

        def sem(name):
            return ctx.enter_context(nc.semaphore(name))

        def each_slot(name):
            return [sem(f"{name}_{s}") for s in range(SLOTS)]

        slot_of = nc.dram_tensor("slot_of", (N, 1), I32).ap()
        hop1 = nc.dram_tensor("hop1", (EP + 1, D), F32).ap()
        hop2 = nc.dram_tensor("hop2", (EP + 1, D), F32).ap()
        xsrc_d = nc.dram_tensor("xsrc_d", (EP, D), F32).ap()
        slots_d = nc.dram_tensor("slots_d", (EP, 1), I32).ap()
        keep_d = nc.dram_tensor("keep_d", (1, EP), BF16).ap()
        low_d = nc.dram_tensor("low_d", (1, EP), BF16).ap()
        irec_d = nc.dram_tensor("irec_d", (EP, 2), I32).ap()
        gidx_d = nc.dram_tensor("gidx_d", (EP, 1), I32).ap()
        frec_d = nc.dram_tensor("frec_d", (EP, 3), F32).ap()

        R = GROUPS
        dsti = sb("dsti", [R, GROUP], I32)
        nexti = sb("nexti", [R, GROUP], I32)
        previ = sb("previ", [R, GROUP], I32)
        keep = sb("keep", [R, GROUP])
        same_next = sb("same_next", [R, GROUP])
        keep_b = sb("keep_b", [R, GROUP], BF16)
        low_b = sb("low_b", [R, GROUP], BF16)
        ones = sb("ones", [P, GROUP])
        cnt = sb("cnt", [R, GROUP])
        whole = sb("whole", [R, GROUP])
        deg = sb("deg", [R, GROUP])
        logd = sb("logd", [R, GROUP])
        rlogd = sb("rlogd", [R, GROUP])
        irec_all = sb("irec_all", [R, GROUP, 2], I32)
        gidx_all = sb("gidx_all", [R, GROUP], I32)
        frec_all = sb("frec_all", [R, GROUP, 3])
        ends = sb("ends", [1, 2, P])
        carry = sb("carry", [1, R + 1])
        carry_col = sb("carry_col", [R, 1])
        fill = sb("fill", [80, N // 80], I32)
        ident = sb("ident", [P, P])
        eps_col = sb("eps_col", [P, 1])
        one_col = sb("one_col", [P, 1])
        sign = sb("sign", [P, 1])
        w1 = sb("w1", [D + 1, D])
        w2 = sb("w2", [D + 1, D])
        b1row = sb("b1row", [1, D])
        b1relu = sb("b1relu", [1, D])
        b2row = sb("b2row", [1, D])
        b2all = sb("b2all", [P, D])
        we = sb("we", [D, D])
        wedge = sb("wedge", [D, D])
        wcat = sb("wcat", [P, 2, D])
        wpd = sb("wpd", [D, D])
        wpdT = sb("wpdT", [D, D])
        weT = sb("weT", [D, P])
        be_col = sb("be_col", [D, 1])
        wpe2 = sb("wpe2", [D, 2, D])
        bpre2 = sb("bpre2", [P, 1])
        bias2 = sb("bias2", [P, 1])
        sbias2 = sb("sbias2", [P, 1])
        wlin = sb("wlin", [D, D])
        wpx = sb("wpx", [D, D])
        wpxT = sb("wpxT", [D, D])
        wps = sb("wps", [P, 6, D])
        wpsT = sb("wpsT", [D, 6, P])
        wsh = sb("wsh", [D, 3, 3, D])
        wsum = sb("wsum", [D, 3, D])
        wshT = sb("wshT", [D, 3, D])
        wshTx = sb("wshTx", [D, D])
        bpost_col = sb("bpost_col", [D, 1])
        blin_row = sb("blin_row", [1, D])
        brow = sb("brow", [1, 3, D])
        crow = sb("crow", [1, D])
        f_ms = sb("f_ms", [P, 3 * D])
        f_xn = sb("f_xn", [P, 3 * D])
        f_h = sb("f_h", [D + 1, 3 * D])
        w_dense = sb("w_dense", [D + 1, D])
        hist_i = sb("hist_i", [P, BINS], I32)
        hist = sb("hist", [P, BINS])
        bins = sb("bins", [P, BINS])
        logb = sb("logb", [P, BINS])
        hl = sb("hl", [P, BINS])
        avg = sb("avg", [P, 8])
        coef = sb("coef", [P, 3])
        two_col = sb("two_col", [P, 2])

        ps = ctx.enter_context(nc.psum_tensor("ps", [P, 8, 512], F32))

        s_init = sem("constants_set")
        s_ident0 = sem("identity_cleared")
        s_ident = sem("identity_set")
        s_ld = sem("setup_loaded")
        s_iota = sem("positions_set")
        s_dv = sem("setup_vector")
        s_pe = sem("setup_products")
        s_ac = sem("setup_scalar")
        s_rec = sem("records_stored")
        s_fill = sem("slots_filled")
        s_def = sem("defaults_stored")
        s_wrow = sem("weight_rows_moved")
        s_wready = sem("weights_ready")
        s_recready = sem("records_ready")
        s_fready = sem("degree_records_ready")

        L = []
        for layer in (1, 2):
            n = lambda t: f"{t}{layer}"
            b = {}
            b["isrc"] = [sb(n(f"isrc{s}_"), [P, TILES], I32) for s in range(SLOTS)]
            b["irec"] = [sb(n(f"irec{s}_"), [P, TILES, 2], I32) for s in range(SLOTS)]
            b["slots"] = [sb(n(f"slots{s}_"), [P, TILES], I32) for s in range(SLOTS)]
            b["keep"] = [sb(n(f"kp{s}_"), [D, GROUP], BF16) for s in range(SLOTS)]
            b["x8"] = [sb(n(f"x8{s}_"), [P, 2 * TILES, D]) for s in range(SLOTS)]
            b["xc"] = sb(n("xc"), [P, 2 * TILES, D])
            b["sq"] = sb(n("sq"), [P, 2 * TILES, D])
            b["h8"] = [sb(n(f"h8{s}_"), [P, 2 * TILES, D]) for s in range(2)]
            b["st"] = sb(n("st"), [P, 4, 2 * TILES])
            b["hT"] = [sb(n(f"hT{s}_"), [D, GROUP]) for s in range(2)]
            b["dT"] = [sb(n(f"dT{s}_"), [D + 1, GROUP]) for s in range(2)]
            b["S"] = [sb(n(f"S{s}_"), [D + 1, GROUP]) for s in range(2)]
            b["z"] = [sb(n(f"z{s}_"), [P, TILES, D]) for s in range(SLOTS)]
            b["o"] = [sb(n(f"o{s}_"), [P, TILES, D]) for s in range(SLOTS)]
            base = 4 * (layer - 1)
            b["pT"], b["pD"], b["pZ"], b["pO"] = (ps[:, base + q, :] for q in range(4))
            for t in ("idx_loaded", "inputs_loaded", "rows_gathered", "slots_moved",
                      "rows_saved", "hop_stored", "dense_stored"):
                b[t] = each_slot(n(t + "_l"))
            for t in ("rows_read", "sumsq_ready", "std_ready", "h_ready", "transposed", "hT_ready",
                      "dT_ready", "scanned", "hop_product", "dense_product", "hop_ready", "dense_ready",
                      "vector_order"):
                b[t] = sem(n(t + "_l"))
            L.append(b)

        c = {}
        c["slots"] = [sb(f"slots3{s}", [P, TILES], I32) for s in range(SLOTS)]
        c["gidx"] = [sb(f"gidx3{s}", [P, TILES], I32) for s in range(SLOTS)]
        c["irec"] = [sb(f"irec3{s}", [P, TILES, 2], I32) for s in range(SLOTS)]
        c["frec"] = [sb(f"frec3{s}", [P, TILES, 3]) for s in range(SLOTS)]
        c["keep"] = [sb(f"keep3{s}", [P, GROUP], BF16) for s in range(SLOTS)]
        c["low"] = [sb(f"low3{s}", [P, GROUP], BF16) for s in range(SLOTS)]
        c["x8"] = L[0]["x8"]
        c["y8"] = L[1]["x8"]
        c["x2"] = [sb(f"x23{s}", [P, 2 * TILES, D]) for s in range(SLOTS)]
        c["xc"] = sb("xc3", [P, 2 * TILES, D])
        c["sq"] = sb("sq3", [P, 2 * TILES, D])
        c["st"] = sb("st3", [P, 4, 2 * TILES])
        c["cat"] = [sb(f"cat3{s}", [P, TILES, 2 * D]) for s in range(2)]
        c["hd"] = [sb(f"hd3{s}", [P, TILES, D]) for s in range(2)]
        c["catT"] = sb("catT3", [P, GROUP])
        c["hdT"] = L[0]["S"] + L[1]["S"]
        c["u1"] = [sb(f"u13{s}", [P, GROUP]) for s in range(2)]
        c["u2"] = [sb(f"u23{s}", [P, GROUP]) for s in range(2)]
        c["r1"] = [sb(f"r13{s}", [P, GROUP]) for s in range(2)]
        c["r2"] = [sb(f"r23{s}", [P, GROUP]) for s in range(2)]
        c["ms"] = sb("ms3", [P, TILES, 2 * D])
        c["m2"] = sb("m23", [P, TILES, D])
        c["var"] = sb("var3", [P, TILES, D])
        c["msT"] = sb("msT3", [P, GROUP])
        c["t1"] = sb("t13", [P, TILES, D])
        c["t2"] = sb("t23", [P, TILES, D])
        c["o1"] = sb("o13", [P, TILES, D])
        c["o"] = [sb(f"o3{s}", [P, TILES, D]) for s in range(SLOTS)]
        pCat, pC, pH, pR, pM = (ps[:, q, :] for q in range(5))
        pF = ps[:, 6:8, :].rearrange("p b (k n) -> p (b k) n", n=256)
        for t in ("idx_loaded", "target_loaded", "degrees_loaded", "inputs_loaded", "ends_gathered",
                  "out_stored"):
            c[t] = each_slot(t + "_3")
        for t in ("summed", "rows_read", "sumsq_ready", "std_ready", "h_ready", "catT_done", "catT_ready", "msg_done", "hdT_done",
                  "hdT_ready", "msg_ready", "scanned", "back_done", "moments_read", "var_ready", "spread_ready",
                  "msT_done", "msT_ready", "final_done", "final_read", "out_ready", "order_a", "order_c", "order_d"):
            c[t] = sem(t + "_3")

        block = ctx.enter_context(nc.Block())

        def grp(ap, i, s, rows=P):
            if isinstance(i, int):
                r0 = (SLOTS * i + s) * GROUP
                return ap[r0:r0 + rows * TILES].rearrange("(p k) f -> p (k f)", k=TILES)
            return ap[bass.ds(i * (SLOTS * GROUP) + s * GROUP, rows * TILES)].rearrange("(p k) f -> p (k f)", k=TILES)

        def last(i, s):
            return isinstance(i, int) and (i, s) == LAST

        def dense_rows(ap, layer, i, s):
            full = not (layer == 2 and last(i, s))
            rows = P if full else DTAIL
            off = (layer - 1) * GROUPS * GROUP
            if isinstance(i, int):
                r0 = off + (SLOTS * i + s) * GROUP
                v = ap[r0:r0 + rows * TILES]
            else:
                v = ap[bass.ds(i * (SLOTS * GROUP) + s * GROUP + off, rows * TILES)]
            return v.rearrange("(p k) f -> p (k f)", k=TILES), rows

        def mask(ap, i, s, parts):
            if isinstance(i, int):
                v = ap[:, (SLOTS * i + s) * GROUP:(SLOTS * i + s + 1) * GROUP]
            else:
                v = ap[:, bass.ds(i * (SLOTS * GROUP) + s * GROUP, GROUP)]
            return v.to_broadcast([parts, GROUP])

        src2 = src.rearrange("(e o) -> e o", o=1)
        col = lambda v: v.rearrange("(p o) -> p o", o=1)
        row = lambda v: v.rearrange("(o f) -> o f", o=1)
        loads = []
        full = (R - 1) * GROUP
        flat = lambda v: v.rearrange("(r c) -> r c", c=GROUP)
        loads += [(dsti[0:R - 1, :], flat(dst[0:full])),
                  (dsti[R - 1:R, 0:E - full], row(dst[full:E])),
                  (nexti[0:R - 1, :], flat(dst[1:full + 1])),
                  (nexti[R - 1:R, 0:E - full - 1], row(dst[full + 1:E])),
                  (previ[0:1, 1:GROUP], row(dst[0:GROUP - 1])),
                  (previ[1:R - 1, :], flat(dst[GROUP - 1:full - 1])),
                  (previ[R - 1:R, 0:E - full + 1], row(dst[full - 1:E]))]
        wloads = [(w1[0:D, :], W1), (w1[D:D + 1, :], row(b1)), (w2[0:D, :], W2), (w2[D:D + 1, :], row(b2)),
                  (b1row[:, :], row(b1)), (b2row[:, :], row(b2)), (b2all[:, :], row(b2).to_broadcast([P, D])),
                  (we[:, :], W_e), (wedge[:, :], W_pre[2 * D:3 * D, :]), (be_col[:, :], col(b_e)),
                  (wcat[0:D, 0, :], W_pre[D:2 * D, :]), (wcat[0:D, 1, :], W_pre[D:2 * D, :]),
                  (wpd[:, :], W_pre[0:D, :]), (wpe2[:, 0, :], W_pre[2 * D:3 * D, :]),
                  (wpe2[:, 1, :], W_pre[2 * D:3 * D, :]), (bpre2[0:D, :], col(b_pre)), (bpre2[D:P, :], col(b_pre)),
                  (wlin[:, :], W_lin), (wpx[:, :], W_post[0:D, :]), (bpost_col[:, :], col(b_post)),
                  (blin_row[:, :], row(b_lin)), (hist_i[:, :], row(deg_hist).to_broadcast([P, BINS]))]
        MEAN, MIN, MAX, STD = range(4)
        post = lambda j, a: W_post[D + (j * 4 + a) * D:D + (j * 4 + a + 1) * D, :]
        for j in range(3):
            for q, (a0, a1) in enumerate(((MEAN, STD), (MAX, MIN))):
                wloads += [(wps[0:D, 3 * q + j, :], post(j, a0)), (wps[D:P, 3 * q + j, :], post(j, a1))]
            for a in (MEAN, MIN, MAX):
                wloads.append((wsh[:, j, a, :], post(j, a)))

        @block.sync
        def _(sp):
            sp.wait_ge(s_init, 3)
            with nc.allow_non_contiguous_dma(reason="columns of a bias"):
                for d, v in loads + wloads:
                    sp.dma_start(d, v).then_inc(s_ld, 16)
            sp.wait_ge(s_recready, 1)
            sp.wait_ge(s_iota, 1)
            sp.dma_start(keep_d.rearrange("o (r c) -> (o r) c", c=GROUP), keep_b[:, :]).then_inc(s_rec, 16)
            sp.dma_start(low_d.rearrange("o (r c) -> (o r) c", c=GROUP), low_b[:, :]).then_inc(s_rec, 16)
            sp.dma_start(irec_d.rearrange("(r c) f -> r (c f)", c=GROUP),
                         irec_all[:, :, :].rearrange("r c f -> r (c f)")).then_inc(s_rec, 16)
            sp.dma_start(gidx_d.rearrange("(r c) o -> r (c o)", c=GROUP), gidx_all[:, :]).then_inc(s_rec, 16)
            sp.wait_ge(s_rec, 64)

            for layer in (1, 2):
                b = L[layer - 1]

                def step(i, s):
                    rows = TAIL if last(i, s) else P
                    if layer == 1:
                        need(sp, b["rows_gathered"][s], 64 * i)
                        need(sp, b["slots_moved"][s], 64 * i)
                        settle(sp)
                        sp.dma_start(b["irec"][s][:, :, :].rearrange("p k f -> p (k f)"),
                                     grp(irec_d, i, s)).then_inc(b["idx_loaded"][s], 16)
                    else:
                        need(sp, b["slots_moved"][s], 64 * i)
                        settle(sp)
                    sp.dma_start(b["isrc"][s][0:rows, :], grp(src2, i, s, rows)).then_inc(b["idx_loaded"][s], 16)
                    need(sp, b["dense_stored"][s], 16 * i)
                    settle(sp)
                    v, r = dense_rows(x, layer, i, s)
                    sp.dma_start(b["x8"][s][0:r, TILES:2 * TILES, :].rearrange("p k f -> p (k f)"),
                                 v).then_inc(b["inputs_loaded"][s], 16)
                    need(sp, b["scanned"], (SLOTS * i + s) - SLOTS + 1)
                    settle(sp)
                    sp.dma_start(b["keep"][s][:, :], mask(keep_d, i, s, D)).then_inc(b["inputs_loaded"][s], 16)

                turns(sp, step)

            for s in range(SLOTS):
                sp.wait_ge(L[0]["rows_saved"][s], 16 * uses(s))
                sp.wait_ge(L[0]["dense_stored"][s], 16 * uses(s))
                sp.wait_ge(L[1]["dense_stored"][s], 16 * uses(s))
                sp.wait_ge(L[1]["rows_saved"][s], 16 * uses(s))
                sp.wait_ge(L[1]["hop_stored"][s], 16 * uses(s))
            sp.wait_ge(s_fready, 1)
            sp.dma_start(frec_d.rearrange("(r c) f -> r (c f)", c=GROUP),
                         frec_all[:, :, :].rearrange("r c f -> r (c f)")).then_inc(s_rec, 16)
            sp.wait_ge(s_rec, 80)

            def degrees(i, s):
                need(sp, c["out_ready"], (SLOTS * i + s) - SLOTS + 1)
                settle(sp)
                sp.dma_start(c["frec"][s][:, :, :].rearrange("p k f -> p (k f)"),
                             grp(frec_d, i, s)).then_inc(c["degrees_loaded"][s], 16)

            def targets(i, s):
                need(sp, c["out_stored"][s], 64 * i)
                settle(sp)
                sp.dma_start(c["irec"][s][:, :, :].rearrange("p k f -> p (k f)"),
                             grp(irec_d, i, s)).then_inc(c["target_loaded"][s], 16)

            def step3(i, s):
                need(sp, c["ends_gathered"][s], 128 * i)
                settle(sp)
                sp.dma_start(c["gidx"][s][:, :], grp(gidx_d, i, s)).then_inc(c["idx_loaded"][s], 16)
                sp.dma_start(c["slots"][s][:, :], grp(slots_d, i, s)).then_inc(c["idx_loaded"][s], 16)
                need(sp, c["summed"], (SLOTS * i + s) - SLOTS + 1)
                settle(sp)
                flat3 = lambda t: t.rearrange("p k f -> p (k f)")
                sp.dma_start(flat3(c["x8"][s][:, 0:TILES, :]), grp(xsrc_d, i, s)).then_inc(c["inputs_loaded"][s], 16)
                sp.dma_start(flat3(c["y8"][s][:, TILES:2 * TILES, :]), grp(hop2, i, s)).then_inc(c["inputs_loaded"][s], 16)
                need(sp, c["catT_done"], (SLOTS * i + s) - 1)
                settle(sp)
                rows = TAIL if last(i, s) else P
                sp.dma_start(c["cat"][s % 2][0:rows, :, D:2 * D],
                             grp(edge_attr, i, s, rows).rearrange("p (k f) -> p k f", f=D)).then_inc(
                                 c["inputs_loaded"][s], 16)
                need(sp, c["scanned"], 2 * (SLOTS * i + s - SLOTS + 1))
                settle(sp)
                sp.dma_start(c["keep"][s][:, :], mask(keep_d, i, s, P)).then_inc(c["inputs_loaded"][s], 16)
                sp.dma_start(c["low"][s][:, :], mask(low_d, i, s, P)).then_inc(c["inputs_loaded"][s], 16)
                if before(i, s, SCAN):
                    degrees(*before(i, s, SCAN))
                if before(i, s, FINISH):
                    targets(*before(i, s, FINISH))

            turns(sp, step3, 9)
            after_last(degrees, SCAN)
            after_last(targets, FINISH)
            for s in range(SLOTS):
                sp.wait_ge(c["out_stored"][s], 64 * uses(s))

        @block.gpsimd
        def _(pool):
            pool.iota(irec_all[:, :, 1], pattern=[[1, GROUP]], base=0, channel_multiplier=GROUP).then_inc(s_iota, 1)
            pool.memset(ident[:, :], 0.0).then_inc(s_ident0, 1)
            pool.wait_ge(s_ident0, 1)
            pool.affine_select(out=ident[:, :], in_=ident[:, :], compare_op=ALU.not_equal, fill=1.0, base=0,
                               pattern=[[-1, P]], channel_multiplier=1).then_inc(s_ident, 1)
            pool.iota(bins[:, :], pattern=[[1, BINS]], base=1, channel_multiplier=0,
                      allow_small_or_imprecise_dtypes=True).then_inc(s_iota, 1)

            def gather(dest, table, index, done):
                pool.indirect_dma_start(dest, None, table, bass.IndirectOffsetOnAxis(ap=index.bitcast(U32), axis=0)
                                        ).then_inc(done, 16)

            def scatter(table, index, source, done):
                pool.indirect_dma_start(table, bass.IndirectOffsetOnAxis(ap=index.bitcast(U32), axis=0), source,
                                        None, bounds_check=N - 1, oob_is_err=False).then_inc(done, 16)

            pool.wait_ge(s_fill, 16)
            b = L[0]

            def step1(i, s):
                pool.wait_ge(b["idx_loaded"][s], 32 * i + 32)
                need(pool, b["rows_saved"][s], 16 * i)
                need(pool, b["rows_read"], (SLOTS * i + s) - SLOTS + 1)
                settle(pool)
                for k in range(TILES):
                    gather(b["x8"][s][:, k, :], x, b["isrc"][s][:, k:k + 1], b["rows_gathered"][s])
                for k in range(TILES):
                    scatter(slot_of, b["irec"][s][:, k, 0:1], b["irec"][s][:, k, 1:2], b["slots_moved"][s])

            turns(pool, step1)

            q = L[1]
            for s in range(SLOTS):
                pool.wait_ge(b["slots_moved"][s], 64 * uses(s))
                pool.wait_ge(b["hop_stored"][s], 16 * uses(s))
            pool.wait_ge(s_def, 32)

            def rows2(i, s):
                pool.wait_ge(q["slots_moved"][s], 64 * i + 64)
                need(pool, q["transposed"], (SLOTS * i + s) - SLOTS + 1)
                settle(pool)
                for k in range(TILES):
                    gather(q["x8"][s][:, k, :], hop1, q["slots"][s][:, k:k + 1], q["rows_gathered"][s])

            def step2(i, s):
                pool.wait_ge(q["idx_loaded"][s], 16 * i + 16)
                need(pool, q["rows_gathered"][s], 64 * i)
                need(pool, q["rows_saved"][s], 16 * i)
                settle(pool)
                for k in range(TILES):
                    gather(q["slots"][s][:, k:k + 1], slot_of, q["isrc"][s][:, k:k + 1], q["slots_moved"][s])
                if before(i, s):
                    rows2(*before(i, s))

            turns(pool, step2)
            rows2(*LAST)

            for s in range(SLOTS):
                pool.wait_ge(q["hop_stored"][s], 16 * uses(s))
                pool.wait_ge(L[0]["dense_stored"][s], 16 * uses(s))
                pool.wait_ge(q["dense_stored"][s], 16 * uses(s))

            def out3(i, s):
                pool.wait_ge(c["out_ready"], SLOTS * i + s + 1)
                pool.wait_ge(c["target_loaded"][s], 16 * i + 16)
                settle(pool)
                for k in range(TILES):
                    scatter(out, c["irec"][s][:, k, 0:1], c["o"][s][:, k, :], c["out_stored"][s])

            def step3(i, s):
                pool.wait_ge(c["idx_loaded"][s], 32 * i + 32)
                need(pool, c["summed"], (SLOTS * i + s) - SLOTS + 1)
                settle(pool)
                for k in range(TILES):
                    gather(c["y8"][s][:, k, :], hop2, c["slots"][s][:, k:k + 1], c["ends_gathered"][s])
                for k in range(TILES):
                    gather(c["x8"][s][:, TILES + k, :], x, c["gidx"][s][:, k:k + 1], c["ends_gathered"][s])
                if before(i, s, SCATTER):
                    out3(*before(i, s, SCATTER))

            turns(pool, step3, 9)
            after_last(out3, SCATTER)

        @block.tensor
        def _(pe):
            pe.wait_ge(s_ident, 1)
            nw = 16 * (len(loads) + len(wloads))
            pe.wait_ge(s_ld, nw)
            T = nc.tensor.transpose
            M = nc.tensor.matmul

            def mm(o, l, r, start=True, stop=True):
                return M(o, l, r, start=start, stop=stop)

            T(ps[0:D, 0, 0:D], we[:, :], ident[0:D, 0:D])
            T(ps[0:D, 0, D:2 * D], wpd[:, :], ident[0:D, 0:D])
            T(ps[0:D, 0, 2 * D:3 * D], wpx[:, :], ident[0:D, 0:D])
            for j in range(6):
                ins = T(ps[0:D, 1 + j // 3, (j % 3) * P:(j % 3 + 1) * P], wps[:, j, :], ident[:, :])
            ins.then_inc(s_pe, 1)
            pe.wait_ge(s_dv, 1)
            for j in range(3):
                mm(ps[0:D, 3, j * D:(j + 1) * D], wsum[:, j, :], wpdT[:, :])
            mm(ps[:, 4, 0:1], wpe2[:, :, :].rearrange("p a f -> p (a f)"), be_col[:, :])
            mm(ps[:, 4, 64:128], weT[:, :], wedge[:, :])
            for j in range(3):
                mm(ps[:, 5, j * D:(j + 1) * D], wpsT[:, j, :], wlin[:, :])
            for j in range(3):
                mm(ps[:, 6, j * D:(j + 1) * D], wpsT[:, 3 + j, :], wlin[:, :])
            mm(ps[0:1, 7, 0:D], bpost_col[:, :], wlin[:, :]).then_inc(s_pe, 1)
            pe.wait_ge(s_dv, 2)
            mm(ps[0:D, 0, 0:D], wshTx[:, :], wlin[:, :])
            for j in range(1, 3):
                mm(ps[0:D, 0, j * D:(j + 1) * D], wshT[:, j, :], wlin[:, :])
            mm(ps[0:D, 1, 0:D], wpxT[:, :], wlin[:, :])
            for j in range(3):
                ins = mm(ps[0:1, 2, 0:D], coef[:, j:j + 1], f_ms[:, j * D:(j + 1) * D], start=j == 0, stop=j == 2)
            ins.then_inc(s_pe, 1)
            pe.wait_ge(s_dv, 3)
            T(ps[0:1, 3, 0:R], cnt[:, GROUP - 1:GROUP], ident[0:R, 0:R])
            T(ps[0:1, 4, 0:R], whole[:, GROUP - 1:GROUP], ident[0:R, 0:R]).then_inc(s_pe, 1)
            pe.wait_ge(s_dv, 4)
            T(ps[0:R, 5, 0:1], carry[0:1, 0:R], ident[0:1, 0:1]).then_inc(s_pe, 1)
            pe.wait_ge(s_dv, 5)
            pe.wait_ge(s_wrow, 32)

            for layer in (1, 2):
                b = L[layer - 1]
                w = (w1, w2)[layer - 1]

                def products(i, s):
                    g = SLOTS * i + s
                    pe.wait_ge(b["dT_ready"], g + 1)
                    need(pe, b["dense_ready"], g)
                    for k in range(TILES):
                        ins = mm(b["pO"][:, k * D:(k + 1) * D], b["dT"][s % 2][:, k * P:(k + 1) * P], w_dense[:, :])
                    ins.then_inc(b["dense_product"], 1)
                    pe.wait_ge(b["scanned"], g + 1)
                    need(pe, b["hop_ready"], g)
                    for k in range(TILES):
                        ins = mm(b["pZ"][:, k * D:(k + 1) * D], b["S"][s % 2][:, k:GROUP:TILES], w[:, :])
                    ins.then_inc(b["hop_product"], 1)

                def step(i, s):
                    g = SLOTS * i + s
                    pe.wait_ge(b["h_ready"], g + 1)
                    if layer == 2:
                        pe.wait_ge(b["rows_gathered"][s], 64 * i + 64)
                    need(pe, b["dT_ready"], g)
                    settle(pe)
                    for k in range(TILES):
                        T(b["pD"][0:D, k * P:(k + 1) * P], b["h8"][s % 2][:, TILES + k, :], ident[:, :])
                    rows = b["h8"] if layer == 1 else b["x8"]
                    for k in range(TILES):
                        ins = T(b["pT"][0:D, k:GROUP:TILES], rows[s % len(rows)][:, k, :], ident[:, :])
                    ins.then_inc(b["transposed"], 1)
                    if before(i, s):
                        products(*before(i, s))

                turns(pe, step)
                products(*LAST)

            for s in range(SLOTS):
                pe.wait_ge(L[1]["hop_stored"][s], 16 * uses(s))
                pe.wait_ge(L[1]["dense_stored"][s], 16 * uses(s))

            def finals(i, s):
                g = SLOTS * i + s
                pe.wait_ge(c["spread_ready"], g + 1)
                need(pe, c["msT_ready"], g)
                for k in range(TILES):
                    ins = T(pM[:, k * P:(k + 1) * P], c["ms"][:, k, :], ident[:, :])
                ins.then_inc(c["msT_done"], 1)
                pe.wait_ge(c["msT_ready"], g + 1)
                pe.wait_ge(c["hdT_ready"], g + 1)
                need(pe, c["final_read"], g)
                for k in range(TILES):
                    mm(pF[:, k, 0:3 * D], c["r2"][s % 2][:, k:GROUP:TILES], f_xn[:, :], stop=False)
                    mm(pF[:, k, 0:3 * D], c["hdT"][s][:, k * P:(k + 1) * P], f_h[:, :], start=False, stop=False)
                    ins = mm(pF[:, k, 0:3 * D], c["msT"][:, k * P:(k + 1) * P], f_ms[:, :], start=False)
                ins.then_inc(c["final_done"], 1)

            def back(i, s):
                g = SLOTS * i + s
                pe.wait_ge(c["scanned"], 2 * g + 2)
                need(pe, c["moments_read"], g)
                for k in range(TILES):
                    ins = T(pR[:, k * P:(k + 1) * P], c["r1"][s % 2][:, k:GROUP:TILES], ident[:, :])
                ins.then_inc(c["back_done"], 1)

            def step3(i, s):
                g = SLOTS * i + s
                if before(i, s, SCAN):
                    back(*before(i, s, SCAN))
                pe.wait_ge(c["h_ready"], g + 1)
                pe.wait_ge(c["inputs_loaded"][s], 80 * i + 80)
                need(pe, c["catT_ready"], g)
                for k in range(TILES):
                    ins = T(pCat[:, k:GROUP:TILES], c["cat"][s % 2][:, k, :], ident[:, :])
                ins.then_inc(c["catT_done"], 1)
                need(pe, c["hdT_ready"], g)
                settle(pe)
                for k in range(TILES):
                    ins = T(pH[0:D, k * P:(k + 1) * P], c["hd"][s % 2][:, k, :], ident[:, :])
                ins.then_inc(c["hdT_done"], 1)
                pe.wait_ge(c["catT_ready"], g + 1)
                need(pe, c["msg_ready"], g)
                mm(pC[:, :], wcat[:, :, :].rearrange("p a f -> p (a f)"), c["catT"][:, :]).then_inc(c["msg_done"], 1)
                if before(i, s, SPREAD):
                    finals(*before(i, s, SPREAD))

            turns(pe, step3, 9)
            after_last(back, SCAN)
            after_last(finals, SPREAD)

        @block.scalar
        def _(act):
            A = nc.scalar.activation
            act.wait_ge(s_init, 4)
            act.dma_start(slot_of.rearrange("(p c) o -> p (c o)", p=80), fill[:, :]).then_inc(s_fill, 16)
            act.wait_ge(s_iota, 2)
            A(logb[:, :], bins[:, :], ACT.Ln).then_inc(s_ac, 1)
            A(two_col[:, 0:1], one_col[:, :], ACT.Ln, bias=one_col[:, :]).then_inc(s_ac, 1)
            A(two_col[:, 1:2], one_col[:, :], ACT.Sqrt, bias=eps_col[:, :], scale=0.0).then_inc(s_ac, 1)
            act.wait_ge(s_dv, 2)
            act.dma_start(hop1[DEFAULT:DEFAULT + 1, :], b1relu[:, :]).then_inc(s_def, 16)
            act.dma_start(hop2[DEFAULT:DEFAULT + 1, :], b2row[:, :]).then_inc(s_def, 16)
            act.dma_start(f_h[D:D + 1, :], brow[:, :, :].rearrange("o a f -> o (a f)")).then_inc(s_wrow, 16)
            act.wait_ge(s_dv, 5)
            act.dma_start(w_dense[D:D + 1, :], crow[:, :]).then_inc(s_wrow, 16)
            act.wait_ge(s_dv, 6)
            A(logd[:, :], deg[:, :], ACT.Ln, bias=one_col[0:R, :]).then_inc(s_ac, 1)

            flat3 = lambda t: t.rearrange("p k f -> p (k f)")
            for layer in (1, 2):
                b = L[layer - 1]

                def stores(i, s):
                    g = SLOTS * i + s
                    act.wait_ge(b["hop_product"], g + 1)
                    need(act, b["hop_stored"][s], 16 * i)
                    A(flat3(b["z"][s][:, :, :]), b["pZ"][:, 0:TILES * D],
                      ACT.Relu if layer == 1 else ACT.Copy).then_inc(b["hop_ready"], 1)
                    act.wait_ge(b["hop_ready"], g + 1)
                    act.dma_start(grp((hop1, hop2)[layer - 1], i, s), flat3(b["z"][s][:, :, :])).then_inc(
                        b["hop_stored"][s], 16)
                    act.wait_ge(b["dense_ready"], g + 1)
                    v, r = dense_rows(out, layer, i, s)
                    act.dma_start(v, flat3(b["o"][s][0:r, :, :])).then_inc(b["dense_stored"][s], 16)

                def step(i, s):
                    g = SLOTS * i + s
                    lo = 0 if layer == 1 else TILES
                    if layer == 1:
                        act.wait_ge(b["rows_gathered"][s], 64 * i + 64)
                        act.dma_start(grp(xsrc_d, i, s), flat3(b["x8"][s][:, 0:TILES, :])).then_inc(
                            b["rows_saved"][s], 16)
                    else:
                        act.wait_ge(b["slots_moved"][s], 64 * i + 64)
                        act.dma_start(grp(slots_d, i, s), b["slots"][s][:, :]).then_inc(b["rows_saved"][s], 16)
                    act.wait_ge(b["sumsq_ready"], g + 1)
                    A(b["st"][:, 2, lo:], b["st"][:, 1, lo:], ACT.Sqrt, bias=eps_col[:, :],
                      scale=1.0 / D).then_inc(b["std_ready"], 1)
                    act.wait_ge(b["transposed"], g + 1)
                    need(act, b["scanned"], g - 1)
                    A(b["hT"][s % 2][:, :], b["pT"][0:D, :], ACT.Copy).then_inc(b["hT_ready"], 1)
                    need(act, b["dense_product"], g - 1)
                    A(b["dT"][s % 2][0:D, :], b["pD"][0:D, :], ACT.Copy).then_inc(b["dT_ready"], 1)
                    if before(i, s):
                        stores(*before(i, s))

                turns(act, step)
                stores(*LAST)

            def spread(i, s):
                g = SLOTS * i + s
                act.wait_ge(c["var_ready"], g + 1)
                A(c["ms"][:, :, D:2 * D], c["var"][:, :, :], ACT.Sqrt).then_inc(c["spread_ready"], 1)
                act.wait_ge(c["msT_done"], g + 1)
                need(act, c["final_done"], g)
                A(c["msT"][:, :], pM[:, :], ACT.Copy).then_inc(c["msT_ready"], 1)

            def step3(i, s):
                g = SLOTS * i + s
                act.wait_ge(c["sumsq_ready"], g + 1)
                A(c["st"][:, 2, :], c["st"][:, 1, :], ACT.Sqrt, bias=eps_col[:, :], scale=1.0 / D).then_inc(
                    c["std_ready"], 1)
                act.wait_ge(c["catT_done"], g + 1)
                need(act, c["msg_done"], g)
                A(c["catT"][:, :], pCat[:, :], ACT.Copy).then_inc(c["catT_ready"], 1)
                act.wait_ge(c["hdT_done"], g + 1)
                need(act, c["final_done"], g - SLOTS + 1)
                A(c["hdT"][s][0:D, :], pH[0:D, :], ACT.Copy).then_inc(c["hdT_ready"], 1)
                act.wait_ge(c["msg_done"], g + 1)
                need(act, c["scanned"], 2 * g - 2)
                A(c["u1"][s % 2][0:D, :], pC[0:D, :], ACT.Identity, bias=bias2[0:D, :])
                A(c["u1"][s % 2][D:P, :], pC[D:P, :], ACT.Square, bias=bias2[D:P, :])
                A(c["u2"][s % 2][:, :], pC[:, :], ACT.Identity, bias=sbias2[:, :], scale=sign[:, :]).then_inc(
                    c["msg_ready"], 1)
                if before(i, s, SPREAD):
                    spread(*before(i, s, SPREAD))

            turns(act, step3, 9)
            after_last(spread, SPREAD)

        @block.vector
        def _(dve):
            V = nc.vector
            V.memset(dsti[:, :], FAR).then_inc(s_init, 1)
            V.memset(nexti[:, :], FAR).then_inc(s_init, 1)
            V.memset(previ[:, :], -1).then_inc(s_init, 1)
            V.memset(one_col[:, :], 1.0)
            V.memset(eps_col[:, :], EPS)
            V.memset(fill[:, :], DEFAULT).then_inc(s_init, 1)
            V.memset(ones[:, :], 1.0)
            V.memset(sign[0:D, :], 1.0)
            V.memset(sign[D:P, :], -1.0)
            V.memset(weT[:, 0:D], 0.0)
            V.memset(coef[:, :], 0.0)
            V.memset(brow[:, :, :], 0.0)
            for t in (L[0]["isrc"], L[1]["isrc"]):
                for s in range(SLOTS):
                    V.memset(t[s][:, :], 0)
            for b in L:
                for s in range(2):
                    V.memset(b["dT"][s % 2][D:D + 1, :], 1.0)
                    V.memset(b["S"][s % 2][D:D + 1, :], 1.0)
            chain = Order(dve, s_wready, 0)
            chain.begin(0)
            link = chain.link
            link(V.memset(carry[:, :], 0.0))
            nw = 16 * (len(loads) + len(wloads))
            dve.wait_ge(s_ld, nw)
            dve.wait_ge(s_pe, 1)
            V.tensor_copy(weT[:, D:P], ps[0:D, 0, 0:D])
            V.tensor_copy(wpdT[:, :], ps[0:D, 0, D:2 * D])
            V.tensor_copy(wpxT[:, :], ps[0:D, 0, 2 * D:3 * D])
            V.tensor_copy(wpsT[:, 0:3, :].rearrange("p a f -> p (a f)"), ps[0:D, 1, 0:3 * P])
            V.tensor_copy(wpsT[:, 3:6, :].rearrange("p a f -> p (a f)"), ps[0:D, 2, 0:3 * P])
            link(V.tensor_tensor(wsum[:, :, :], wsh[:, :, MEAN, :], wsh[:, :, MIN, :], ALU.add))
            V.tensor_tensor(wsum[:, :, :], wsum[:, :, :], wsh[:, :, MAX, :], ALU.add).then_inc(s_dv, 1)
            dve.wait_ge(s_ac, 3)
            link(V.tensor_copy(hist[:, :], hist_i[:, :]))
            link(V.tensor_tensor(hl[:, :], hist[:, :], logb[:, :], ALU.mult))
            link(V.tensor_reduce(avg[:, 0:1], hl[:, :], AX, ALU.add))
            link(V.tensor_reduce(avg[:, 1:2], hist[:, :], AX, ALU.add))
            link(V.reciprocal(avg[:, 2:3], avg[:, 1:2]))
            link(V.tensor_tensor(avg[:, 3:4], avg[:, 0:1], avg[:, 2:3], ALU.mult))
            link(V.reciprocal(avg[:, 4:5], avg[:, 3:4]))
            link(V.reciprocal(avg[:, 5:6], two_col[:, 0:1]))
            link(V.tensor_copy(coef[D:P, 0:1], two_col[D:P, 1:2]))
            link(V.tensor_tensor(avg[:, 6:7], two_col[:, 0:1], avg[:, 4:5], ALU.mult))
            link(V.tensor_tensor(avg[:, 7:8], avg[:, 3:4], avg[:, 5:6], ALU.mult))
            link(V.tensor_tensor(coef[D:P, 1:2], avg[D:P, 6:7], two_col[D:P, 1:2], ALU.mult))
            link(V.tensor_tensor(coef[D:P, 2:3], avg[D:P, 7:8], two_col[D:P, 1:2], ALU.mult))
            dve.wait_ge(s_pe, 2)
            V.tensor_copy(wshT[:, :, :].rearrange("p a f -> p (a f)"), ps[0:D, 3, 0:3 * D])
            V.tensor_tensor(wshTx[:, :], ps[0:D, 3, 0:D], wpxT[:, :], ALU.add)
            link(V.tensor_tensor(bias2[:, :], ps[:, 4, 0:1], bpre2[:, :], ALU.add))
            V.tensor_tensor(sbias2[:, :], bias2[:, :], sign[:, :], ALU.mult)
            for a in range(2):
                V.tensor_copy(wcat[D:P, a, :], ps[D:P, 4, D:2 * D])
            V.tensor_copy(f_ms[:, :], ps[:, 5, 0:3 * D])
            V.tensor_scalar(f_xn[:, :], ps[:, 6, 0:3 * D], sign[:, :], None, ALU.mult)
            V.tensor_scalar(b1relu[:, :], b1row[:, :], 0.0, None, ALU.max)
            V.tensor_tensor(brow[:, 0, :], ps[0:1, 7, 0:D], blin_row[:, :], ALU.add).then_inc(s_dv, 1)
            link(V.tensor_tensor(keep[:, :], dsti[:, :], previ[:, :], ALU.is_equal))
            link(V.tensor_tensor(same_next[:, :], dsti[:, :], nexti[:, :], ALU.is_equal))
            V.tensor_copy(keep_b[:, :], keep[:, :])
            V.tensor_scalar(low_b[:, :], keep[:, :], -1.0, -LOW, ALU.add, ALU.mult)
            V.tensor_scalar(gidx_all[:, :], dsti[:, :], float(N - 1), None, ALU.min)
            V.scalar_tensor_tensor(irec_all[:, :, 0], same_next[:, :], float(FAR), dsti[:, :], ALU.mult,
                                   ALU.add).then_inc(s_recready, 1)
            V.tensor_tensor_scan(cnt[:, :], keep[:, :], ones[0:R, :], 0.0, ALU.mult, ALU.add)
            V.tensor_tensor_scan(whole[:, :], keep[:, :], keep[:, :], 1.0, ALU.mult, ALU.mult).then_inc(s_dv, 1)
            dve.wait_ge(s_pe, 4)
            V.tensor_copy(ends[:, 0, 0:R], ps[0:1, 3, 0:R])
            link(V.tensor_copy(ends[:, 1, 0:R], ps[0:1, 4, 0:R]))
            V.tensor_tensor_scan(carry[:, 1:R + 1], ends[:, 1, 0:R], ends[:, 0, 0:R], 0.0, ALU.mult,
                                 ALU.add).then_inc(s_dv, 1)
            V.tensor_copy(f_h[0:D, :], ps[0:D, 0, 0:3 * D])
            V.tensor_copy(w_dense[0:D, :], ps[0:D, 1, 0:D])
            V.tensor_tensor(crow[:, :], ps[0:1, 2, 0:D], brow[:, 0, :], ALU.add).then_inc(s_dv, 1)
            dve.wait_ge(s_pe, 5)
            link(V.tensor_copy(carry_col[:, :], ps[0:R, 5, 0:1]))
            link(V.scalar_tensor_tensor(deg[:, :], whole[:, :], carry_col[:, :], cnt[:, :], ALU.mult, ALU.add))
            V.reciprocal(frec_all[:, :, 0], deg[:, :]).then_inc(s_dv, 1)
            dve.wait_ge(s_ac, 4)
            link(V.reciprocal(rlogd[:, :], logd[:, :]))
            V.tensor_scalar(frec_all[:, :, 1], logd[:, :], avg[0:R, 4:5], None, ALU.mult)
            V.tensor_scalar(frec_all[:, :, 2], rlogd[:, :], avg[0:R, 3:4], None, ALU.mult).then_inc(s_fready, 1)

            def wide(t, n):
                return t.rearrange("p (k o) -> p k o", o=1).to_broadcast([P, n, D])

            def moments(o, b, rows, lo, n, g, read, sumsq, std, meanwhile=None):
                hi = lo + n
                o.link(V.tensor_reduce(b["st"][:, 0, lo:hi], rows, AX, ALU.add))
                o.link(V.tensor_scalar(b["st"][:, 3, lo:hi], b["st"][:, 0, lo:hi], -1.0 / D, None, ALU.mult))
                ins = V.tensor_tensor(b["xc"][:, lo:hi, :], rows, wide(b["st"][:, 3, lo:hi], n), ALU.add)
                ins.then_inc(read, 1)
                dve.wait_ge(read, g + 1)
                o.link(V.tensor_tensor(b["sq"][:, lo:hi, :], b["xc"][:, lo:hi, :], b["xc"][:, lo:hi, :], ALU.mult))
                V.tensor_reduce(b["st"][:, 1, lo:hi], b["sq"][:, lo:hi, :], AX, ALU.add).then_inc(sumsq, 1)
                if meanwhile:
                    meanwhile()
                dve.wait_ge(std, g + 1)
                o.link(V.reciprocal(b["st"][:, 3, lo:hi], b["st"][:, 2, lo:hi]))

            for layer in (1, 2):
                b = L[layer - 1]
                o = Order(dve, b["vector_order"], 5)
                lo, n = (0, 2 * TILES) if layer == 1 else (TILES, TILES)

                def results(i, s):
                    g = SLOTS * i + s
                    dve.wait_ge(b["hT_ready"], g + 1)
                    dve.wait_ge(b["inputs_loaded"][s], 32 * i + 32)
                    need(dve, b["scanned"], g)
                    need(dve, b["hop_product"], g - 1)
                    state = b["S"][1 - s % 2][0:D, GROUP - 1:GROUP] if before(i, s) else 0.0
                    V.tensor_tensor_scan(b["S"][s % 2][0:D, :], b["keep"][s][:, :], b["hT"][s % 2][:, :], state,
                                         ALU.mult, ALU.add).then_inc(b["scanned"], 1)
                    dve.wait_ge(b["dense_product"], g + 1)
                    need(dve, b["dense_stored"][s], 16 * i)
                    V.tensor_tensor(b["o"][s][:, :, :],
                                    b["pO"][:, 0:TILES * D].rearrange("p (k f) -> p k f", f=D),
                                    b["x8"][s][:, TILES:2 * TILES, :], ALU.add).then_inc(b["dense_ready"], 1)

                def step(i, s):
                    g = SLOTS * i + s
                    o.begin(g)
                    dve.wait_ge(b["inputs_loaded"][s], 32 * i + 32)
                    dx = b["x8"][s][:, TILES:2 * TILES, :]
                    bb = b2all[:, :].rearrange("p (o f) -> p o f", o=1).to_broadcast([P, TILES, D])
                    o.link(V.tensor_tensor(dx, dx, bb, ALU.add))
                    if layer == 1:
                        dve.wait_ge(b["rows_gathered"][s], 64 * i + 64)
                    moments(o, b, b["x8"][s][:, lo:lo + n, :], lo, n, g, b["rows_read"], b["sumsq_ready"],
                            b["std_ready"])
                    need(dve, b["transposed"], g - 1)
                    V.scalar_tensor_tensor(b["h8"][s % 2][:, lo:lo + n, :], b["xc"][:, lo:lo + n, :], 0.0,
                                           wide(b["st"][:, 3, lo:lo + n], n), ALU.max, ALU.mult).then_inc(
                                               b["h_ready"], 1)
                    o.end()
                    if before(i, s):
                        results(*before(i, s))

                turns(dve, step)
                results(*LAST)

            oa, oc, od = (Order(dve, c[t], k) for t, k in (("order_a", 4), ("order_c", 2), ("order_d", 1)))
            deg_of = lambda s, q: c["frec"][s][:, :, q:q + 1]

            def spread(i, s):
                g = SLOTS * i + s
                oc.begin(g)
                dve.wait_ge(c["back_done"], g + 1)
                dve.wait_ge(c["degrees_loaded"][s], 16 * i + 16)
                need(dve, c["msT_done"], g)
                ins = V.tensor_tensor(c["ms"][:, :, :], pR[:, :].rearrange("p (k f) -> p k f", f=2 * D),
                                      deg_of(s, 0).to_broadcast([P, TILES, 2 * D]), ALU.mult)
                ins.then_inc(c["moments_read"], 1)
                dve.wait_ge(c["moments_read"], g + 1)
                oc.link(V.tensor_tensor(c["m2"][:, :, :], c["ms"][:, :, 0:D], c["ms"][:, :, 0:D], ALU.mult))
                need(dve, c["spread_ready"], g)
                oc.link(V.tensor_tensor(c["m2"][:, :, :], c["ms"][:, :, D:2 * D], c["m2"][:, :, :], ALU.subtract))
                V.tensor_scalar(c["var"][:, :, :], c["m2"][:, :, :], 0.0, EPS, ALU.max, ALU.add).then_inc(
                    c["var_ready"], 1)
                oc.end()

            def scans(i, s):
                g = SLOTS * i + s
                dve.wait_ge(c["msg_ready"], g + 1)
                dve.wait_ge(c["inputs_loaded"][s], 80 * i + 80)
                need(dve, c["scanned"], 2 * g)
                need(dve, c["back_done"], g - 1)
                need(dve, c["final_done"], g - 1)
                first = before(i, s) is None
                V.tensor_tensor_scan(c["r1"][s % 2][:, :], c["keep"][s][:, :], c["u1"][s % 2][:, :],
                                     0.0 if first else c["r1"][1 - s % 2][:, GROUP - 1:GROUP],
                                     ALU.mult, ALU.add).then_inc(c["scanned"], 1)
                V.tensor_tensor_scan(c["r2"][s % 2][:, :], c["low"][s][:, :], c["u2"][s % 2][:, :],
                                     LOW if first else c["r2"][1 - s % 2][:, GROUP - 1:GROUP],
                                     ALU.add, ALU.max).then_inc(c["scanned"], 1)

            def final(i, s):
                g = SLOTS * i + s
                od.begin(g)
                dve.wait_ge(c["final_done"], g + 1)
                need(dve, c["out_stored"][s], 64 * i)
                need(dve, c["out_ready"], g)
                V.tensor_tensor(c["o1"][:, :, :], pF[:, :, 0:D], c["x2"][s][:, TILES:2 * TILES, :], ALU.add)
                V.tensor_tensor(c["t1"][:, :, :], pF[:, :, D:2 * D], deg_of(s, 1).to_broadcast([P, TILES, D]),
                                ALU.mult)
                ins = V.tensor_tensor(c["t2"][:, :, :], pF[:, :, 2 * D:3 * D],
                                      deg_of(s, 2).to_broadcast([P, TILES, D]), ALU.mult)
                ins.then_inc(c["final_read"], 1)
                dve.wait_ge(c["final_read"], g + 1)
                od.link(V.tensor_tensor(c["t1"][:, :, :], c["t1"][:, :, :], c["t2"][:, :, :], ALU.add))
                V.tensor_tensor(c["o"][s][:, :, :], c["o1"][:, :, :], c["t1"][:, :, :], ALU.add).then_inc(
                    c["out_ready"], 1)
                od.end()

            def step3(i, s):
                g = SLOTS * i + s
                oa.begin(g)
                dve.wait_ge(c["inputs_loaded"][s], 80 * i + 80)
                dve.wait_ge(c["ends_gathered"][s], 128 * i + 128)
                need(dve, c["out_ready"], g - SLOTS + 1)
                V.tensor_tensor(c["x2"][s][:, :, :], c["x8"][s][:, :, :], c["y8"][s][:, :, :], ALU.add).then_inc(
                    c["summed"], 1)
                dve.wait_ge(c["summed"], g + 1)
                moments(oa, c, c["x2"][s][:, :, :], 0, 2 * TILES, g, c["rows_read"], c["sumsq_ready"],
                        c["std_ready"],
                        lambda: scans(*before(i, s, SCAN)) if before(i, s, SCAN) else None)
                need(dve, c["hdT_done"], g - 1)
                V.scalar_tensor_tensor(c["cat"][s % 2][:, :, 0:D], c["xc"][:, 0:TILES, :], 0.0,
                                       wide(c["st"][:, 3, 0:TILES], TILES), ALU.max, ALU.mult)
                V.scalar_tensor_tensor(c["hd"][s % 2][:, :, :], c["xc"][:, TILES:, :], 0.0,
                                       wide(c["st"][:, 3, TILES:], TILES), ALU.max, ALU.mult).then_inc(c["h_ready"], 1)
                oa.end()
                if before(i, s, SPREAD):
                    spread(*before(i, s, SPREAD))
                if before(i, s, FINISH):
                    final(*before(i, s, FINISH))

            turns(dve, step3, 9)
            after_last(scans, SCAN)
            spread(*divmod(GROUPS - 2, SLOTS))
            final(*divmod(GROUPS - 3, SLOTS))
            spread(*LAST)
            after_last(final, FINISH - 1)


_INS = ['x', 'src', 'dst', 'edge_attr_64', 'L0_gnn_W1', 'L0_gnn_b1', 'L0_gnn_W2', 'L0_gnn_b2', 'L1_gnn_deg_hist',
        'L1_gnn_W_e', 'L1_gnn_b_e', 'L1_gnn_W_pre', 'L1_gnn_b_pre', 'L1_gnn_W_post', 'L1_gnn_b_post',
        'L1_gnn_W_lin', 'L1_gnn_b_lin']


def kernel(**inputs):
    import numpy as _np
    import concourse.bacc as _bacc
    from concourse import mybir as _mybir
    from concourse.bass_utils import run_bass_kernel_spmd as _run

    nc = _bacc.Bacc("TRN2", target_bir_lowering=False, num_devices=1)
    arrays, args = {}, []
    for name in _INS:
        a = _np.ascontiguousarray(inputs[name])
        arrays[f"in_{name}_dram"] = a
        args.append(nc.dram_tensor(f"in_{name}_dram", a.shape, _mybir.dt.from_np(a.dtype), kind="ExternalInput").ap())
    args.append(nc.dram_tensor("out_0_dram", (N, D), _mybir.dt.float32, kind="ExternalOutput").ap())
    gnn(nc, *args)
    r = _run(nc, [arrays], core_ids=[0])
    return r.results[0]["out_0_dram"]
```

```python
import concourse.bass as bass
from concourse import mybir
from contextlib import ExitStack

F32, F16, BF16 = mybir.dt.float32, mybir.dt.float16, mybir.dt.bfloat16
I32, U32 = mybir.dt.int32, mybir.dt.uint32
ALU = mybir.AluOpType
ACT = mybir.ActivationFunctionType
AX = mybir.AxisListType.X

N, E, D, P = 100000, 50000, 64, 128
TILES = 4
GROUP = TILES * P
GROUPS = -(-E // GROUP)
SLOTS = 4
LAST = divmod(GROUPS - 1, SLOTS)
HALF = TILES // 2
RESULT = 2
SAVE, STORE = 2, 5
FOUND, GATHER, GROW = 1, 2, 3
SCAN, SPREAD, FINISH, SCATTER = 1, 2, 3, 5
EP = GROUPS * GROUP
TAIL = (E - (GROUPS - 1) * GROUP) // TILES
DTAIL = (N - (2 * GROUPS - 1) * GROUP) // TILES
DEFAULT = EP
FAR = 1 << 20
LOW = -3.0e38
CHUNKS = 4
WIDE = -(-N // (P * CHUNKS))
COLS = CHUNKS * WIDE
BANK = COLS // 2
WARM = 4
EPS = 1e-5
SYNC_WEIGHTS = 14
BINS = 32
assert GROUPS % SLOTS == 2 and 0 < DTAIL <= P and (E - (GROUPS - 1) * GROUP) % TILES == 0


def need(eng, sem, value):
    if not isinstance(value, int) or value > 0:
        eng.wait_ge(sem, value)


def settle(eng):
    eng.nop(nofuse=True)


class Order:

    def __init__(self, eng, sem, n, start=0):
        self.eng, self.sem, self.n, self.start = eng, sem, n, start

    def begin(self, turn):
        self.base, self.k = turn * self.n + self.start, 0

    def link(self, ins):
        ins.then_inc(self.sem, 1)
        self.k += 1
        self.eng.wait_ge(self.sem, self.base + self.k)

    def end(self):
        assert self.k == self.n, (self.k, self.n)


def turns(eng, step, first=SLOTS + 1, last=1):
    for g in range(first):
        step(*divmod(g, SLOTS))
    start, at = divmod(first, SLOTS)
    rounds = (GROUPS - first - last) // SLOTS
    with eng.Fori(start, start + rounds) as i:
        for s in range(at, at + SLOTS):
            step(i + s // SLOTS if s >= SLOTS else i, s % SLOTS)
    for g in range(first + rounds * SLOTS, GROUPS):
        step(*divmod(g, SLOTS))


def before(i, s, n=1):
    back = -((s - n) // SLOTS)
    if isinstance(i, int) and i < back:
        return None
    return (i - back if back else i), (s - n) % SLOTS


def following(i, s):
    if isinstance(i, int) and (i, s) == LAST:
        return None
    return (i, s + 1) if s + 1 < SLOTS else (i + 1, 0)


def after_last(stage, lag):
    for g in range(GROUPS - lag, GROUPS):
        stage(*divmod(g, SLOTS))


def late(i, s):
    return isinstance(i, int) and SLOTS * i + s >= GROUPS - SLOTS


def uses(s):
    return len(range(s, GROUPS, SLOTS))


def gnn(nc, x, src, dst, edge_attr, W1, b1, W2, b2, deg_hist, W_e, b_e, W_pre, b_pre,
        W_post, b_post, W_lin, b_lin, out):
    with ExitStack() as ctx:
        def sb(name, shape, dt=F32):
            return ctx.enter_context(nc.sbuf_tensor(name, shape, dt))

        def sem(name):
            return ctx.enter_context(nc.semaphore(name))

        def each_slot(name):
            return [sem(f"{name}_{s}") for s in range(SLOTS)]

        hop1 = nc.dram_tensor("hop1", (EP + 1, D), F32).ap()
        hop2 = nc.dram_tensor("hop2", (EP + 1, D), F32).ap()
        xboth_d = nc.dram_tensor("xboth_d", (GROUPS * P, 2 * TILES * D), F32).ap()
        slots_d = nc.dram_tensor("slots_d", (EP, 1), I32).ap()
        masks_d = nc.dram_tensor("masks_d", (1, 2 * EP), BF16).ap()
        sidx_d = nc.dram_tensor("sidx_d", (EP, 1), I32).ap()
        rec_d = nc.dram_tensor("rec_d", (EP, 5), I32).ap()
        low512_d = nc.dram_tensor("low512_d", (1, EP), F16).ap()
        frec_d = nc.dram_tensor("frec_d", (EP, 3), F32).ap()

        R = GROUPS
        big = [sb(f"big{n}", [P, GROUP]) for n in range(12)]
        cnt, whole, deg, logd, rlogd, keep, same_next = (t[0:R, :] for t in big[0:7])
        dsti, nexti, previ, srci = (t[0:R, :].bitcast(I32) for t in big[8:12])
        masks_b = sb("masks_b", [R, 2, GROUP], BF16)
        ones = sb("ones", [P, COLS])
        sidx_all = sb("sidx_all", [R, GROUP], I32)
        part_i = sb("part_i", [R, GROUP], I32)
        rec_all = sb("rec_all", [R, GROUP, 5], I32)
        low512_all = sb("low512_all", [R, GROUP], F16)
        frec_all = sb("frec_all", [R, GROUP, 3])
        ends = sb("ends", [1, 2, P])
        first_idx = sb("first_idx", [P, 2, SLOTS, TILES], I32)
        carry = sb("carry", [1, R + 1])
        carry_col = sb("carry_col", [R, 1])
        upper = sb("upper", [P, P])
        iota_hi = sb("iota_hi", [P, COLS], F16)
        row_of = sb("row_of", [P, CHUNKS])
        hot_lo = [sb(f"hot_lo{k}", [P, P], F16) for k in range(TILES)]
        hot_hi = [sb(f"hot_hi{k}", [P, COLS], F16) for k in range(TILES)]
        hot = [sb(f"hot{s}", [P, CHUNKS, GROUP], F16) for s in range(2)]
        slot_f = sb("slot_f", [P, TILES])
        table_hi = sb("table_hi", [P, CHUNKS, WIDE], F16)
        table_lo = sb("table_lo", [P, CHUNKS, WIDE], F16)
        ident = sb("ident", [P, P])
        eps_col = sb("eps_col", [P, 1])
        one_col = sb("one_col", [P, 1])
        sign = sb("sign", [P, 1])
        w1 = sb("w1", [D + 1, D])
        w2 = sb("w2", [D + 1, D])
        b1row = sb("b1row", [1, D])
        b1relu = sb("b1relu", [1, D])
        b2all = sb("b2all", [P, D])
        we = sb("we", [D, D])
        wcat = sb("wcat", [P, 2, D])
        wpd = sb("wpd", [D, D])
        wpdT = sb("wpdT", [D, D])
        weT = sb("weT", [D, P])
        be_col = sb("be_col", [D, 1])
        wpe2 = sb("wpe2", [D, 2, D])
        bpre2 = sb("bpre2", [P, 1])
        bias2 = sb("bias2", [P, 1])
        sbias2 = sb("sbias2", [P, 1])
        wlin = sb("wlin", [D, D])
        wpx = sb("wpx", [D, D])
        wpxT = sb("wpxT", [D, D])
        wps = sb("wps", [P, 6, D])
        wpsT = sb("wpsT", [D, 6, P])
        wsh = sb("wsh", [D, 3, 3, D])
        wsum = sb("wsum", [D, 3, D])
        wshT = sb("wshT", [D, 3, D])
        wshTx = sb("wshTx", [D, D])
        bpost_col = sb("bpost_col", [D, 1])
        blin_row = sb("blin_row", [1, D])
        brow = sb("brow", [1, 3, D])
        crow = sb("crow", [1, D])
        f_ms = sb("f_ms", [P, 3 * D])
        f_xn = sb("f_xn", [P, 3 * D])
        f_h = sb("f_h", [D + 1, 3 * D])
        w_dense = sb("w_dense", [D + 1, D])
        hist_i = sb("hist_i", [P, BINS], I32)
        hist = sb("hist", [P, BINS])
        bins = sb("bins", [P, BINS])
        logb = sb("logb", [P, BINS])
        hl = sb("hl", [P, BINS])
        avg = sb("avg", [P, 8])
        coef = sb("coef", [P, 3])
        two_col = sb("two_col", [P, 2])

        ps = ctx.enter_context(nc.psum_tensor("ps", [P, 8, 512], F32))

        s_init = sem("constants_set")
        s_ident0 = sem("identity_cleared")
        s_ident = sem("identity_set")
        s_first = sem("first_ends_loaded")
        s_ld = sem("edges_loaded")
        s_wld = sem("weights_loaded")
        s_iota = sem("positions_set")
        s_dv = sem("setup_vector")
        s_pe = sem("setup_products")
        s_ac = sem("setup_scalar")
        s_rec = sem("records_stored")
        s_tab = sem("slot_table")
        s_tabpe = sem("slot_sums")
        s_def = sem("defaults_stored")
        s_wrow = sem("weight_rows_moved")
        s_wready = sem("weights_ready")
        s_recready = sem("records_ready")
        s_fready = sem("degree_records_ready")

        L = []
        for layer in (1, 2):
            n = lambda t: f"{t}{layer}"
            b = {}
            b["rec"] = [sb(n(f"rec{s}_"), [P, TILES, 5], I32) for s in range(SLOTS)]
            b["xd"] = [sb(n(f"xd{s}_"), [P, HALF, D]) for s in range(SLOTS)]
            if layer == 2:
                b["slots"] = [sb(n(f"slots{s}_"), [P, TILES], I32) for s in range(SLOTS)]
                b["low512"] = [sb(n(f"low512{s}_"), [P, GROUP], F16) for s in range(SLOTS)]
            b["keep"] = [sb(n(f"kp{s}_"), [D, GROUP], BF16) for s in range(SLOTS)]
            b["x8"] = [sb(n(f"x8{s}_"), [P, 2 * TILES, D]) for s in range(SLOTS)]
            b["xc"] = sb(n("xc"), [P, 2 * TILES, D])
            b["sq"] = sb(n("sq"), [P, 2 * TILES, D])
            b["h8_all"] = sb(n("h8"), [P, 2, 2 * TILES, D])
            b["h8"] = [b["h8_all"][:, s, :, :] for s in range(2)]
            b["st"] = sb(n("st"), [P, 4, 2 * TILES])
            b["hT"] = [sb(n(f"hT{s}_"), [D, GROUP]) for s in range(2)]
            b["dT"] = [sb(n(f"dT{s}_"), [D + 1, GROUP]) for s in range(2)]
            b["S"] = [sb(n(f"S{s}_"), [D + 1, GROUP]) for s in range(2)]
            b["z"] = [sb(n(f"z{s}_"), [P, TILES, D]) for s in range(SLOTS)]
            b["o"] = [sb(n(f"o{s}_"), [P, TILES, D]) for s in range(SLOTS)]
            b["pT"], b["pD"], b["pZ"], b["pO"] = (ps[:, q, :] for q in range(4))
            for t in ("idx_loaded", "inputs_loaded", "rows_gathered", "ends_gathered",
                      "rows_saved", "hop_stored", "dense_stored"):
                b[t] = each_slot(n(t + "_l"))
            for t in ("rows_read", "squared", "std_ready", "h_ready", "transposed", "hT_ready",
                      "dT_ready", "scanned", "hop_product", "dense_product", "hop_ready", "dense_ready",
                      "hot_ready", "counted" if layer == 1 else "looked_up"):
                b[t] = sem(n(t + "_l"))
            L.append(b)

        L[1]["slots_found"] = sem("slots_found")
        pCount = ps[:, 4:6, 0:BANK]
        pFound = ps[:, 4:6, :].rearrange("p b (k n) -> p (b k) n", n=256)

        norm_order, find_order, biased_rows = sem("norm_order"), sem("find_order"), sem("biased_rows")

        c = {}
        c["slots"] = [sb(f"slots3{s}", [P, TILES], I32) for s in range(SLOTS)]
        c["sidx"] = [sb(f"sidx3{s}", [P, TILES], I32) for s in range(SLOTS)]
        c["frec"] = [sb(f"frec3{s}", [P, TILES, 3]) for s in range(SLOTS)]
        c["masks"] = [sb(f"masks3{s}", [P, 2, GROUP], BF16) for s in range(SLOTS)]
        c["x8"] = L[0]["x8"]
        c["y8"] = L[1]["x8"]
        x2_all = sb("x23", [P, SLOTS, 2 * TILES, D])
        c["x2"] = [x2_all[:, s, :, :] for s in range(SLOTS)]
        c["xc"], c["sq"] = L[0]["xc"], L[0]["sq"]
        c["st"] = sb("st3", [P, 4, 2 * TILES])
        c["cat"] = [sb(f"cat3{s}", [P, TILES, 2 * D]) for s in range(2)]
        c["hd"] = [sb(f"hd3{s}", [P, TILES, D]) for s in range(2)]
        c["hdT"] = L[0]["S"] + L[1]["S"]
        c["r2"], c["r1"], c["u1"], c["u2"] = big[0:4], big[4:6], big[6:8], big[8:10]
        c["catT"], c["msT"] = big[10:12]
        c["ms"] = [sb(f"ms3{s}", [P, TILES, 2 * D]) for s in range(2)]
        c["m2"], c["t1"], c["t2"] = L[0]["z"][0:3]
        c["var"] = L[0]["o"][0:2]
        c["o"] = L[1]["z"]
        counts, incl = (x2_all[:, 2 * q:2 * q + 2, :, :].rearrange("p a k f -> p (a k f)")[:, 0:COLS] for q in range(2))
        rank = L[1]["h8_all"][:, :, :, :].rearrange("p a k f -> p (a k f)")[:, 0:COLS]
        filled = L[0]["h8_all"][:, :, :, :].rearrange("p a k f -> p (a k f)")[:, 0:COLS]
        slot_i, slot_hi, slot_lo = rank.bitcast(I32), filled.bitcast(I32), incl.bitcast(I32)
        pCat, pC, pH, pR, pM = (ps[:, q, :] for q in range(5))
        pF = ps[:, 6:8, :].rearrange("p b (k n) -> p (b k) n", n=256)
        for t in ("idx_loaded", "target_loaded", "degrees_loaded", "inputs_loaded", "hop2_gathered",
                  "out_stored"):
            c[t] = each_slot(t + "_3")
        for t in ("summed", "rows_read", "squared", "sumsq_ready", "std_ready", "h_ready", "catT_done",
                  "catT_ready", "msg_done", "hdT_done", "sums_in",
                  "hdT_ready", "msg_ready", "scanned", "back_done", "scaled", "moments_read", "var_ready",
                  "spread_ready",
                  "msT_done", "msT_ready", "final_done", "out_ready", "order_c", "order_d"):
            c[t] = sem(t + "_3")

        block = ctx.enter_context(nc.Block())

        def grp(ap, i, s, rows=P):
            if isinstance(i, int):
                r0 = (SLOTS * i + s) * GROUP
                return ap[r0:r0 + rows * TILES].rearrange("(p k) f -> p (k f)", k=TILES)
            return ap[bass.ds(i * (SLOTS * GROUP) + s * GROUP, rows * TILES)].rearrange("(p k) f -> p (k f)", k=TILES)

        def last(i, s):
            return isinstance(i, int) and (i, s) == LAST

        def dense_rows(ap, layer, i, s):
            full = not (layer == 2 and last(i, s))
            rows = P if full else DTAIL
            off = (layer - 1) * GROUPS * GROUP
            if isinstance(i, int):
                r0 = off + (SLOTS * i + s) * GROUP
                v = ap[r0:r0 + rows * TILES]
            else:
                v = ap[bass.ds(i * (SLOTS * GROUP) + s * GROUP + off, rows * TILES)]
            return v.rearrange("(p k) f -> p (k f)", k=TILES), rows

        def spread_row(ap, i, s, parts, n=GROUP, step=GROUP):
            if isinstance(i, int):
                at = (SLOTS * i + s) * step
                v = ap[:, at:at + n]
            else:
                v = ap[:, bass.ds(i * (SLOTS * step) + s * step, n)]
            return v.to_broadcast([parts, n])

        def both(i, s, lo, hi):
            if isinstance(i, int):
                v = xboth_d[(SLOTS * i + s) * P:(SLOTS * i + s + 1) * P]
            else:
                v = xboth_d[bass.ds(i * (SLOTS * P) + s * P, P)]
            return v[:, lo * D:hi * D]

        col = lambda v: v.rearrange("(p o) -> p o", o=1)
        row = lambda v: v.rearrange("(o f) -> o f", o=1)
        loads = []
        full = (R - 1) * GROUP
        flat = lambda v: v.rearrange("(r c) -> r c", c=GROUP)
        loads += [(dsti[0:R - 1, :], flat(dst[0:full])),
                  (dsti[R - 1:R, 0:E - full], row(dst[full:E])),
                  (nexti[0:R - 1, :], flat(dst[1:full + 1])),
                  (nexti[R - 1:R, 0:E - full - 1], row(dst[full + 1:E])),
                  (previ[0:1, 1:GROUP], row(dst[0:GROUP - 1])),
                  (previ[1:R - 1, :], flat(dst[GROUP - 1:full - 1])),
                  (previ[R - 1:R, 0:E - full + 1], row(dst[full - 1:E])),
                  (srci[0:R - 1, :], flat(src[0:full])),
                  (srci[R - 1:R, 0:E - full], row(src[full:E]))]
        twice = lambda v: v.rearrange("f (o c) -> f o c", o=1).to_broadcast([D, 2, D])
        wloads = [(w1[0:D, :], W1), (w1[D:D + 1, :], row(b1)), (w2[0:D, :], W2), (w2[D:D + 1, :], row(b2)),
                  (b1row[:, :], row(b1)), (b2all[:, :], row(b2).to_broadcast([P, D])),
                  (we[:, :], W_e), (be_col[:, :], col(b_e)),
                  (wcat[0:D, :, :], twice(W_pre[D:2 * D, :])), (wpd[:, :], W_pre[0:D, :]),
                  (wpe2[:, :, :], twice(W_pre[2 * D:3 * D, :])),
                  (bpre2[0:D, :], col(b_pre)), (bpre2[D:P, :], col(b_pre)),
                  (wlin[:, :], W_lin), (wpx[:, :], W_post[0:D, :]), (bpost_col[:, :], col(b_post)),
                  (blin_row[:, :], row(b_lin)), (hist_i[:, :], row(deg_hist).to_broadcast([P, BINS]))]
        MEAN, MIN, MAX, STD = range(4)
        post = W_post[D:13 * D, :].rearrange("(j a f) c -> a f j c", j=3, a=4)
        for q, (a0, a1) in enumerate(((MEAN, STD), (MAX, MIN))):
            wloads += [(wps[0:D, 3 * q:3 * q + 3, :], post[a0]), (wps[D:P, 3 * q:3 * q + 3, :], post[a1])]
        for a in (MEAN, MIN, MAX):
            wloads.append((wsh[:, :, a, :], post[a]))

        @block.sync
        def _(sp):
            def hold(sem, value):
                need(sp, sem, value)
                settle(sp)

            with nc.allow_non_contiguous_dma(reason="four edges on each partition, columns of a bias"):
                for n, v in enumerate((src, dst)):
                    sp.dma_start(first_idx[:, n, :, :], v[0:SLOTS * GROUP].rearrange(
                        "(g p k) -> p g k", p=P, k=TILES)).then_inc(s_first, 16)
                sp.wait_ge(s_init, 4)
                for d, v in loads:
                    sp.dma_start(d, v).then_inc(s_ld, 16)
                for d, v in wloads[:SYNC_WEIGHTS]:
                    sp.dma_start(d, v).then_inc(s_wld, 16)
            sp.wait_ge(s_recready, 1)
            flat2 = lambda v: v.rearrange("(r c) f -> r (c f)", c=GROUP)
            for d, v in ((masks_d.rearrange("o (r c) -> (o r) c", c=2 * GROUP),
                          masks_b[:, :, :].rearrange("r m c -> r (m c)")),
                         (flat2(sidx_d), sidx_all[:, :]),
                         (flat2(rec_d), rec_all[:, :, :].rearrange("r c f -> r (c f)")),
                         (low512_d.rearrange("o (r c) -> (o r) c", c=GROUP), low512_all[:, :])):
                sp.dma_start(d, v).then_inc(s_rec, 16)
            sp.wait_ge(s_rec, 64)
            b, q = L

            flat3 = lambda t: t.rearrange("p k f -> p (k f)")

            def record(b, i, s):
                hold(b["ends_gathered"][s], HALF * 16 * i)
                if b is L[0]:
                    hold(b["rows_gathered"][s], TILES * 16 * i)
                    hold(b["hot_ready"], TILES * (SLOTS * i + s - SLOTS + 1))
                else:
                    hold(b["slots_found"], (SLOTS * i + s) - SLOTS + 1)
                sp.dma_start(flat3(b["rec"][s][:, :, :]), grp(rec_d, i, s)).then_inc(b["idx_loaded"][s], 16)

            def inputs(b, i, s):
                layer = 1 if b is L[0] else 2
                hold(b["dense_ready"], (SLOTS * i + s) - SLOTS + 1)
                hold(b["scanned"], (SLOTS * i + s) - SLOTS + 1)
                v, r = dense_rows(x, layer, i, s)
                sp.dma_start(flat3(b["x8"][s][0:r, TILES:2 * TILES, :]), v).then_inc(b["inputs_loaded"][s], 16)
                sp.dma_start(b["keep"][s][:, :], spread_row(masks_d, i, s, D, GROUP, 2 * GROUP)).then_inc(
                    b["inputs_loaded"][s], 16)

            def save_rows(b, i, s):
                hold(b["rows_gathered"][s], TILES * 16 * (i + 1))
                hold(b["ends_gathered"][s], HALF * 16 * (i + 1))
                if b is L[0]:
                    sp.dma_start(both(i, s, 0, TILES), flat3(b["x8"][s][:, 0:TILES, :])).then_inc(
                        b["rows_saved"][s], 16)
                    sp.dma_start(both(i, s, TILES, TILES + HALF), flat3(b["xd"][s][:, :, :])).then_inc(
                        b["rows_saved"][s], 16)
                else:
                    sp.dma_start(grp(slots_d, i, s), b["slots"][s][:, :]).then_inc(b["rows_saved"][s], 16)
                    sp.dma_start(both(i, s, TILES + HALF, 2 * TILES), flat3(b["xd"][s][:, :, :])).then_inc(
                        b["rows_saved"][s], 16)

            def save_results(b, i, s):
                g = SLOTS * i + s
                hold(b["dense_ready"], g + 1)
                hold(b["hop_ready"], g + 1)
                v, r = dense_rows(out, 1 if b is L[0] else 2, i, s)
                sp.dma_start(v, flat3(b["o"][s][0:r, :, :])).then_inc(b["dense_stored"][s], 16)
                sp.dma_start(grp(hop1 if b is L[0] else hop2, i, s), flat3(b["z"][s][:, :, :])).then_inc(
                    b["hop_stored"][s], 16)

            def step1(i, s):
                record(b, i, s)
                if before(i, s):
                    inputs(b, *before(i, s))
                if before(i, s, SAVE) and not late(*before(i, s, SAVE)):
                    save_rows(b, *before(i, s, SAVE))
                if before(i, s, STORE):
                    save_results(b, *before(i, s, STORE))

            def look(i, s):
                hold(q["hot_ready"], (SLOTS * i + s) - SLOTS + 1)
                sp.dma_start(q["low512"][s][:, :], spread_row(low512_d, i, s, P)).then_inc(q["idx_loaded"][s], 16)
                record(q, i, s)

            turns(sp, step1, 9, SAVE)
            inputs(b, *LAST)
            for s in range(SLOTS):
                look(0, s)
            after_last(lambda i, s: save_rows(b, i, s), SLOTS)
            after_last(lambda i, s: save_results(b, i, s), STORE)

            def later2(i, s):
                inputs(q, i, s)
                if before(i, s, SAVE - 1) and not late(*before(i, s, SAVE - 1)):
                    save_rows(q, *before(i, s, SAVE - 1))
                if before(i, s, STORE):
                    save_results(q, *before(i, s, STORE))

            def step2(i, s):
                if not (isinstance(i, int) and i == 0):
                    look(i, s)
                if before(i, s, GATHER):
                    later2(*before(i, s, GATHER))

            turns(sp, step2, 9)
            after_last(lambda i, s: inputs(q, i, s), GATHER)
            sp.wait_ge(s_fready, 6)
            sp.dma_start(frec_d.rearrange("(r c) f -> r (c f)", c=GROUP),
                         frec_all[:, :, :].rearrange("r c f -> r (c f)")).then_inc(s_rec, 16)

            def slots3(i, s):
                hold(c["hop2_gathered"][s], 64 * i)
                sp.dma_start(c["slots"][s][:, :], grp(slots_d, i, s)).then_inc(c["idx_loaded"][s], 16)

            def early3(i, s):
                hold(c["summed"], (SLOTS * i + s) - SLOTS + 1)
                sp.dma_start(flat3(c["x8"][s][:, :, :]), both(i, s, 0, 2 * TILES)).then_inc(c["inputs_loaded"][s], 16)
                hold(c["scanned"], 2 * (SLOTS * i + s - SLOTS + 1))
                sp.dma_start(c["masks"][s][:, :, :].rearrange("p m c -> p (m c)"),
                             spread_row(masks_d, i, s, P, 2 * GROUP, 2 * GROUP)).then_inc(c["inputs_loaded"][s], 16)

            for s in range(SLOTS):
                sp.wait_ge(q["rows_saved"][s], 32)
                slots3(0, s)
            for g in range(GROUPS - GATHER - STORE, GROUPS - SAVE):
                save_results(q, *divmod(g, SLOTS))
            after_last(lambda i, s: save_rows(q, i, s), SLOTS)
            after_last(lambda i, s: save_results(q, i, s), SAVE)
            for s in range(SLOTS):
                sp.wait_ge(b["rows_saved"][s], 32 * uses(s))
                sp.wait_ge(q["rows_saved"][s], 32 * uses(s))
            for s in range(SLOTS):
                early3(0, s)

            for s in range(SLOTS):
                sp.wait_ge(q["hop_stored"][s], 16 * uses(s))
            sp.wait_ge(s_rec, 80)

            def degrees(i, s):
                hold(c["out_ready"], (SLOTS * i + s) - SLOTS + 1)
                sp.dma_start(c["frec"][s][:, :, :].rearrange("p k f -> p (k f)"),
                             grp(frec_d, i, s)).then_inc(c["degrees_loaded"][s], 16)

            def targets(i, s):
                hold(c["out_stored"][s], 64 * i)
                sp.dma_start(c["sidx"][s][:, :], grp(sidx_d, i, s)).then_inc(c["target_loaded"][s], 16)

            def step3(i, s):
                if not (isinstance(i, int) and i == 0):
                    slots3(i, s)
                    early3(i, s)
                hold(c["summed"], (SLOTS * i + s) - SLOTS + 1)
                sp.dma_start(flat3(c["y8"][s][:, TILES:2 * TILES, :]), grp(hop2, i, s)).then_inc(
                    c["inputs_loaded"][s], 16)
                hold(c["catT_done"], (SLOTS * i + s) - 1)
                rows = TAIL if last(i, s) else P
                sp.dma_start(c["cat"][s % 2][0:rows, :, D:2 * D],
                             grp(edge_attr, i, s, rows).rearrange("p (k f) -> p k f", f=D)).then_inc(
                                 c["inputs_loaded"][s], 16)
                if before(i, s, SCAN):
                    degrees(*before(i, s, SCAN))
                if before(i, s, FINISH):
                    targets(*before(i, s, FINISH))

            turns(sp, step3, 9)
            after_last(degrees, SCAN)
            after_last(targets, FINISH)
            for s in range(SLOTS):
                sp.wait_ge(c["out_stored"][s], 64 * uses(s))

        @block.gpsimd
        def _(pool):
            pool.memset(ident[:, :], 0.0).then_inc(s_ident0, 1)
            pool.wait_ge(s_ident0, 1)
            pool.wait_ge(s_init, 5)
            pool.affine_select(out=ident[:, :], in_=ident[:, :], compare_op=ALU.not_equal, fill=1.0, base=0,
                               pattern=[[-1, P]], channel_multiplier=1).then_inc(s_ident, 1)
            pool.affine_select(out=upper[:, :], in_=ones[:, 0:P], compare_op=ALU.is_ge, fill=0.0, base=0,
                               pattern=[[1, P]], channel_multiplier=-1).then_inc(s_ident, 1)
            pool.iota(iota_hi[:, :], pattern=[[1, COLS]], base=0, channel_multiplier=0,
                      allow_small_or_imprecise_dtypes=True).then_inc(s_iota, 1)
            pool.iota(row_of[:, :], pattern=[[P, CHUNKS]], base=0, channel_multiplier=1,
                      allow_small_or_imprecise_dtypes=True).then_inc(s_iota, 1)
            pool.iota(bins[:, :], pattern=[[1, BINS]], base=1, channel_multiplier=0,
                      allow_small_or_imprecise_dtypes=True).then_inc(s_iota, 1)

            def gather(dest, table, index, done):
                pool.indirect_dma_start(dest, None, table, bass.IndirectOffsetOnAxis(ap=index.bitcast(U32), axis=0)
                                        ).then_inc(done, 16)

            def scatter(table, index, source, done):
                pool.indirect_dma_start(table, bass.IndirectOffsetOnAxis(ap=index.bitcast(U32), axis=0), source,
                                        None, bounds_check=N - 1, oob_is_err=False).then_inc(done, 16)

            b, q = L
            def gather_ends(b, i, s, at):
                for k in range(HALF):
                    index = first_idx[:, 1, s, at + k:at + k + 1] if isinstance(i, int) and i == 0 else (
                        b["rec"][s][:, at + k, 1:2])
                    gather(b["xd"][s][:, k, :], x, index, b["ends_gathered"][s])

            def step1(i, s):
                if isinstance(i, int) and i == 0:
                    pool.wait_ge(s_first, 32)
                else:
                    pool.wait_ge(b["idx_loaded"][s], 16 * i + 16)
                need(pool, b["rows_saved"][s], 32 * i)
                need(pool, b["rows_read"], (SLOTS * i + s) - SLOTS + 1)
                settle(pool)
                for k in range(TILES):
                    index = first_idx[:, 0, s, k:k + 1] if isinstance(i, int) and i == 0 else b["rec"][s][:, k, 0:1]
                    gather(b["x8"][s][:, k, :], x, index, b["rows_gathered"][s])
                if not late(i, s):
                    gather_ends(b, i, s, 0)

            turns(pool, step1, last=SLOTS)
            after_last(lambda i, s: gather_ends(b, i, s, 0), SLOTS)
            for s in range(SLOTS):
                gather_ends(q, 0, s, HALF)
            for s in range(SLOTS):
                pool.wait_ge(b["hop_stored"][s], 16 * uses(s))
            pool.wait_ge(s_def, 32)

            def rows2(i, s):
                pool.wait_ge(q["idx_loaded"][s], 32 * i + 32)
                need(pool, q["rows_saved"][s], 32 * i)
                need(pool, q["transposed"], (SLOTS * i + s) - SLOTS + 1)
                settle(pool)
                if not late(i, s) and not (isinstance(i, int) and i == 0):
                    gather_ends(q, i, s, HALF)
                pool.wait_ge(q["slots_found"], SLOTS * i + s + 1)
                settle(pool)
                for k in range(TILES):
                    gather(q["x8"][s][:, k, :], hop1, q["slots"][s][:, k:k + 1], q["rows_gathered"][s])

            turns(pool, rows2, last=SLOTS)
            after_last(lambda i, s: gather_ends(q, i, s, HALF), SLOTS)

            for s in range(SLOTS):
                pool.wait_ge(q["hop_stored"][s], 16 * uses(s))

            def out3(i, s):
                if not before(i, s):
                    for n in range(SLOTS):
                        pool.wait_ge(L[0]["dense_stored"][n], 16 * uses(n))
                        pool.wait_ge(q["dense_stored"][n], 16 * uses(n))
                pool.wait_ge(c["out_ready"], SLOTS * i + s + 1)
                pool.wait_ge(c["target_loaded"][s], 16 * i + 16)
                settle(pool)
                for k in range(TILES):
                    scatter(out, c["sidx"][s][:, k:k + 1], c["o"][s][:, k, :], c["out_stored"][s])

            def step3(i, s):
                pool.wait_ge(c["idx_loaded"][s], 16 * i + 16)
                need(pool, c["summed"], (SLOTS * i + s) - SLOTS + 1)
                settle(pool)
                for k in range(TILES):
                    gather(c["y8"][s][:, k, :], hop2, c["slots"][s][:, k:k + 1], c["hop2_gathered"][s])
                if before(i, s, SCATTER):
                    out3(*before(i, s, SCATTER))

            turns(pool, step3, 9)
            after_last(out3, SCATTER)

        @block.tensor
        def _(pe):
            pe.wait_ge(s_ident, 2)
            pe.wait_ge(s_iota, 1)
            pe.wait_ge(s_wld, 16 * len(wloads))
            T = nc.tensor.transpose
            M = nc.tensor.matmul

            def mm(o, l, r, start=True, stop=True):
                return M(o, l, r, start=start, stop=stop)

            T(ps[0:D, 0, 0:D], we[:, :], ident[0:D, 0:D])
            T(ps[0:D, 0, D:2 * D], wpd[:, :], ident[0:D, 0:D])
            T(ps[0:D, 0, 2 * D:3 * D], wpx[:, :], ident[0:D, 0:D])
            for j in range(6):
                ins = T(ps[0:D, 1 + j // 3, (j % 3) * P:(j % 3 + 1) * P], wps[:, j, :], ident[:, :])
            ins.then_inc(s_pe, 1)
            pe.wait_ge(s_dv, 1)
            for j in range(3):
                mm(ps[0:D, 3, j * D:(j + 1) * D], wsum[:, j, :], wpdT[:, :])
            mm(ps[:, 4, 0:1], wpe2[:, :, :].rearrange("p a f -> p (a f)"), be_col[:, :])
            mm(ps[:, 4, 64:128], weT[:, :], wpe2[:, 0, :])
            for j in range(3):
                mm(ps[:, 5, j * D:(j + 1) * D], wpsT[:, j, :], wlin[:, :])
            for j in range(3):
                mm(ps[:, 6, j * D:(j + 1) * D], wpsT[:, 3 + j, :], wlin[:, :])
            mm(ps[0:1, 7, 0:D], bpost_col[:, :], wlin[:, :]).then_inc(s_pe, 1)
            pe.wait_ge(s_dv, 2)
            mm(ps[0:D, 0, 0:D], wshTx[:, :], wlin[:, :])
            for j in range(1, 3):
                mm(ps[0:D, 0, j * D:(j + 1) * D], wshT[:, j, :], wlin[:, :])
            mm(ps[0:D, 1, 0:D], wpxT[:, :], wlin[:, :])
            for j in range(3):
                ins = mm(ps[0:1, 2, 0:D], coef[:, j:j + 1], f_ms[:, j * D:(j + 1) * D], start=j == 0, stop=j == 2)
            ins.then_inc(s_pe, 1)
            pe.wait_ge(s_dv, 3)
            T(ps[0:1, 3, 0:R], cnt[:, GROUP - 1:GROUP], ident[0:R, 0:R])
            T(ps[0:1, 4, 0:R], whole[:, GROUP - 1:GROUP], ident[0:R, 0:R]).then_inc(s_pe, 1)
            pe.wait_ge(s_dv, 4)
            T(ps[0:R, 5, 0:1], carry[0:1, 0:R], ident[0:1, 0:1]).then_inc(s_pe, 1)
            pe.wait_ge(s_dv, 5)
            pe.wait_ge(s_wrow, 32)

            def dense_product(b, i, s):
                g = SLOTS * i + s
                pe.wait_ge(b["dT_ready"], g + 1)
                need(pe, b["dense_ready"], g)
                for k in range(TILES):
                    ins = mm(b["pO"][:, k * D:(k + 1) * D], b["dT"][s % 2][:, k * P:(k + 1) * P], w_dense[:, :])
                ins.then_inc(b["dense_product"], 1)

            def transposes(b, i, s):
                g = SLOTS * i + s
                pe.wait_ge(b["h_ready"], g + 1)
                if b is L[1]:
                    pe.wait_ge(b["rows_gathered"][s], TILES * 16 * (i + 1))
                need(pe, b["dT_ready"], g)
                settle(pe)
                for k in range(TILES):
                    T(b["pD"][0:D, k * P:(k + 1) * P], b["h8"][s % 2][:, TILES + k, :], ident[:, :])
                rows = b["h8"] if b is L[0] else b["x8"]
                for k in range(TILES):
                    ins = T(b["pT"][0:D, k:GROUP:TILES], rows[s % len(rows)][:, k, :], ident[:, :])
                ins.then_inc(b["transposed"], 1)

            def hop_product(b, i, s):
                g = SLOTS * i + s
                pe.wait_ge(b["scanned"], g + 1)
                need(pe, b["hop_ready"], g)
                for k in range(TILES):
                    ins = mm(b["pZ"][:, k * D:(k + 1) * D], b["S"][s % 2][:, k:GROUP:TILES],
                             (w1 if b is L[0] else w2)[:, :])
                ins.then_inc(b["hop_product"], 1)

            def count(i, s, tiles):
                g = SLOTS * i + s
                for k in tiles:
                    pe.wait_ge(L[0]["hot_ready"], TILES * g + k + 1)
                    for h in range(2):
                        ins = mm(pCount[:, h, :], hot_lo[k][:, :], hot_hi[k][:, h * BANK:(h + 1) * BANK],
                                 start=isinstance(i, int) and g + k == 0, stop=last(i, s) and k == TILES - 1)
                    ins.then_inc(L[0]["counted"], 1)

            def look_up(i, s):
                g = SLOTS * i + s
                q = L[1]
                pe.wait_ge(q["hot_ready"], g + 1)
                need(pe, q["slots_found"], g)
                for k in range(TILES):
                    for ch in range(CHUNKS):
                        ohc = hot[s % 2][:, ch, k:GROUP:TILES]
                        mm(pFound[:, k, 0:WIDE], ohc, table_hi[:, ch, :], start=ch == 0, stop=False)
                        ins = mm(pFound[:, k, 0:WIDE], ohc, table_lo[:, ch, :], start=False, stop=ch == CHUNKS - 1)
                ins.then_inc(q["looked_up"], 1)

            def keep_warm():
                for _ in range(WARM):
                    mm(ps[:, 7, :], iota_hi[:, 0:P], iota_hi[:, 0:GROUP])

            def step1(i, s):
                count(i, s, range(HALF))
                if before(i, s, RESULT):
                    hop_product(L[0], *before(i, s, RESULT))
                count(i, s, range(HALF, TILES))
                transposes(L[0], i, s)
                if before(i, s):
                    dense_product(L[0], *before(i, s))
                keep_warm()

            def rest(b):
                after_last(lambda i, s: hop_product(b, i, s), RESULT)
                dense_product(b, *LAST)

            turns(pe, step1, 9)

            pe.wait_ge(s_tab, 1)
            for h in range(2):
                mm(ps[:, 6 + h, 0:BANK], upper[:, :], counts[:, h * BANK:(h + 1) * BANK])
                ins = mm(ps[:, 4 + h, 0:BANK], ones[:, 0:P], counts[:, h * BANK:(h + 1) * BANK])
            ins.then_inc(s_tabpe, 1)
            rest(L[0])
            pe.wait_ge(L[0]["hop_ready"], GROUPS)
            pe.wait_ge(L[0]["dense_ready"], GROUPS)
            pe.wait_ge(s_tab, 2)

            def grow(i, s):
                if before(i, s, RESULT):
                    hop_product(L[1], *before(i, s, RESULT))
                transposes(L[1], i, s)
                if before(i, s):
                    dense_product(L[1], *before(i, s))

            def step2(i, s):
                look_up(i, s)
                if before(i, s, GROW):
                    grow(*before(i, s, GROW))

            turns(pe, step2, 9)
            after_last(grow, GROW)
            rest(L[1])

            for s in range(SLOTS):
                pe.wait_ge(L[1]["hop_stored"][s], 16 * uses(s))
                pe.wait_ge(L[1]["dense_stored"][s], 16 * uses(s))

            def spread_transposes(i, s):
                g = SLOTS * i + s
                pe.wait_ge(c["spread_ready"], g + 1)
                need(pe, c["msT_ready"], g)
                for k in range(TILES):
                    ins = T(pM[:, k * P:(k + 1) * P], c["ms"][s % 2][:, k, :], ident[:, :])
                ins.then_inc(c["msT_done"], 1)

            def finals(i, s):
                g = SLOTS * i + s
                pe.wait_ge(c["msT_ready"], g + 1)
                pe.wait_ge(c["hdT_ready"], g + 1)
                need(pe, c["out_ready"], g)
                for k in range(TILES):
                    mm(pF[:, k, 0:3 * D], c["r2"][s][:, k:GROUP:TILES], f_xn[:, :], stop=False)
                    mm(pF[:, k, 0:D], ident[:, :], c["x2"][s][:, TILES + k, :], start=False, stop=False)
                    mm(pF[:, k, 0:3 * D], c["hdT"][s][:, k * P:(k + 1) * P], f_h[:, :], start=False, stop=False)
                    ins = mm(pF[:, k, 0:3 * D], c["msT"][:, k * P:(k + 1) * P], f_ms[:, :], start=False)
                ins.then_inc(c["final_done"], 1)

            def back(i, s):
                g = SLOTS * i + s
                pe.wait_ge(c["scanned"], 2 * g + 2)
                need(pe, c["moments_read"], g)
                for k in range(TILES):
                    ins = T(pR[:, k * P:(k + 1) * P], c["r1"][s % 2][:, k:GROUP:TILES], ident[:, :])
                ins.then_inc(c["back_done"], 1)

            def step3(i, s):
                g = SLOTS * i + s
                if before(i, s, FINISH):
                    finals(*before(i, s, FINISH))
                if before(i, s, SPREAD):
                    spread_transposes(*before(i, s, SPREAD))
                pe.wait_ge(c["h_ready"], g + 1)
                pe.wait_ge(c["inputs_loaded"][s], 64 * i + 64)
                need(pe, c["catT_ready"], g)
                for k in range(TILES):
                    ins = T(pCat[:, k:GROUP:TILES], c["cat"][s % 2][:, k, :], ident[:, :])
                ins.then_inc(c["catT_done"], 1)
                need(pe, c["hdT_ready"], g)
                settle(pe)
                for k in range(TILES):
                    ins = T(pH[0:D, k * P:(k + 1) * P], c["hd"][s % 2][:, k, :], ident[:, :])
                ins.then_inc(c["hdT_done"], 1)
                if before(i, s, SCAN):
                    back(*before(i, s, SCAN))
                pe.wait_ge(c["catT_ready"], g + 1)
                need(pe, c["msg_ready"], g)
                mm(pC[:, :], wcat[:, :, :].rearrange("p a f -> p (a f)"), c["catT"][:, :]).then_inc(c["msg_done"], 1)

            turns(pe, step3, 9)
            finals(*divmod(GROUPS - 3, SLOTS))
            spread_transposes(*divmod(GROUPS - 2, SLOTS))
            back(*LAST)
            finals(*divmod(GROUPS - 2, SLOTS))
            spread_transposes(*LAST)
            finals(*LAST)

        @block.scalar
        def _(act):
            A = nc.scalar.activation
            with nc.allow_non_contiguous_dma(reason="columns of a bias"):
                act.wait_ge(s_ld, 16 * len(loads))
                for d, v in wloads[SYNC_WEIGHTS:]:
                    act.dma_start(d, v).then_inc(s_wld, 16)
            act.wait_ge(s_init, 4)
            act.wait_ge(s_iota, 3)
            A(logb[:, :], bins[:, :], ACT.Ln).then_inc(s_ac, 1)
            A(two_col[:, 0:1], one_col[:, :], ACT.Ln, bias=one_col[:, :]).then_inc(s_ac, 1)
            A(two_col[:, 1:2], one_col[:, :], ACT.Sqrt, bias=eps_col[:, :], scale=0.0).then_inc(s_ac, 1)
            act.wait_ge(s_dv, 2)
            act.dma_start(hop1[DEFAULT:DEFAULT + 1, :], b1relu[:, :]).then_inc(s_def, 16)
            act.dma_start(hop2[DEFAULT:DEFAULT + 1, :], b2all[0:1, :]).then_inc(s_def, 16)
            act.dma_start(f_h[D:D + 1, :], brow[:, :, :].rearrange("o a f -> o (a f)")).then_inc(s_wrow, 16)
            act.wait_ge(s_dv, 5)
            act.dma_start(w_dense[D:D + 1, :], crow[:, :]).then_inc(s_wrow, 16)

            flat3 = lambda t: t.rearrange("p k f -> p (k f)")

            def sums_of_squares(b, lo, g, between):
                act.wait_ge(b["rows_read"], g + 1)
                for k in range(lo, 2 * TILES):
                    ins = A(b["sq"][:, k, :], b["xc"][:, k, :], ACT.Square, accum_out=b["st"][:, 1, k:k + 1])
                ins.then_inc(b["squared"], 1)
                act.wait_ge(b["squared"], g + 1)
                A(b["st"][:, 2, lo:], b["st"][:, 1, lo:], ACT.Sqrt, bias=eps_col[:, :],
                  scale=1.0 / D).then_inc(b["std_ready"], 1)
                between()

            def roots(b, lo, g, between=None):
                act.wait_ge(b["rows_read"], g + 1)
                A(b["sq"][:, lo:, :], b["xc"][:, lo:, :], ACT.Square).then_inc(b["squared"], 1)
                if between:
                    between()
                act.wait_ge(b["sumsq_ready"], g + 1)
                A(b["st"][:, 2, lo:], b["st"][:, 1, lo:], ACT.Sqrt, bias=eps_col[:, :],
                  scale=1.0 / D).then_inc(b["std_ready"], 1)

            for layer in (1, 2):
                b = L[layer - 1]

                def stores(i, s):
                    g = SLOTS * i + s
                    act.wait_ge(b["hop_product"], g + 1)
                    need(act, b["hop_stored"][s], 16 * i)
                    A(flat3(b["z"][s][:, :, :]), b["pZ"][:, 0:TILES * D],
                      ACT.Relu if layer == 1 else ACT.Copy).then_inc(b["hop_ready"], 1)

                def step(i, s):
                    g = SLOTS * i + s
                    lo = 0 if layer == 1 else TILES
                    sums_of_squares(b, lo, g, lambda: evacuate(*before(i, s)) if before(i, s) else None)
                    if before(i, s, RESULT + 1):
                        stores(*before(i, s, RESULT + 1))
                    if layer == 2 and isinstance(i, int) and SLOTS * i + s == 2:
                        act.wait_ge(s_fready, 1)
                        A(logd[:, :], deg[:, :], ACT.Ln, bias=one_col[0:R, :]).then_inc(s_ac, 1)

                def evacuate(i, s):
                    g = SLOTS * i + s
                    act.wait_ge(b["transposed"], g + 1)
                    need(act, b["scanned"], g - 1)
                    A(b["hT"][s % 2][:, :], b["pT"][0:D, :], ACT.Copy).then_inc(b["hT_ready"], 1)
                    need(act, b["dense_product"], g - 1)
                    A(b["dT"][s % 2][0:D, :], b["pD"][0:D, :], ACT.Copy).then_inc(b["dT_ready"], 1)

                turns(act, step, 9)
                evacuate(*LAST)
                after_last(stores, RESULT + 1)

            def scaled(i, s):
                g = SLOTS * i + s
                act.wait_ge(c["back_done"], g + 1)
                act.wait_ge(c["degrees_loaded"][s], 16 * i + 16)
                need(act, c["msT_done"], g - 1)
                for k in range(TILES):
                    ins = A(c["ms"][s % 2][:, k, :], pR[:, k * P:(k + 1) * P], ACT.Copy, scale=c["frec"][s][:, k, 0:1])
                ins.then_inc(c["scaled"], 1)
                act.wait_ge(c["scaled"], g + 1)
                need(act, c["var_ready"], g)
                A(c["m2"][:, :, :], c["ms"][s % 2][:, :, 0:D], ACT.Square).then_inc(c["moments_read"], 1)

            def spread_root(i, s):
                act.wait_ge(c["var_ready"], SLOTS * i + s + 1)
                A(c["ms"][s % 2][:, :, D:2 * D], c["var"][s % 2][:, :, :], ACT.Sqrt).then_inc(c["spread_ready"], 1)

            def spread_out(i, s):
                g = SLOTS * i + s
                act.wait_ge(c["msT_done"], g + 1)
                need(act, c["final_done"], g)
                A(c["msT"][:, :], pM[:, :], ACT.Copy).then_inc(c["msT_ready"], 1)

            def sums_in(i, s):
                g = SLOTS * i + s
                act.wait_ge(c["msg_done"], g + 1)
                need(act, c["scanned"], 2 * g - 2)
                A(c["u1"][s % 2][0:D, :], pC[0:D, :], ACT.Identity, bias=bias2[0:D, :])
                A(c["u1"][s % 2][D:P, :], pC[D:P, :], ACT.Square, bias=bias2[D:P, :]).then_inc(c["sums_in"], 1)

            def extremes_in(i, s):
                A(c["u2"][s % 2][:, :], pC[:, :], ACT.Identity, bias=sbias2[:, :], scale=sign[:, :]).then_inc(
                    c["msg_ready"], 1)

            def step3(i, s):
                g = SLOTS * i + s

                def between():
                    if before(i, s, SCAN):
                        extremes_in(*before(i, s, SCAN))
                    if before(i, s, SPREAD):
                        spread_root(*before(i, s, SPREAD))

                if before(i, s, SCAN):
                    sums_in(*before(i, s, SCAN))
                roots(c, 0, g, between)
                if before(i, s, SPREAD):
                    spread_out(*before(i, s, SPREAD))
                act.wait_ge(c["catT_done"], g + 1)
                need(act, c["msg_done"], g)
                A(c["catT"][:, :], pCat[:, :], ACT.Copy).then_inc(c["catT_ready"], 1)
                if before(i, s, SCAN):
                    scaled(*before(i, s, SCAN))
                act.wait_ge(c["hdT_done"], g + 1)
                need(act, c["final_done"], g - SLOTS + 1)
                A(c["hdT"][s][0:D, :], pH[0:D, :], ACT.Copy).then_inc(c["hdT_ready"], 1)

            def rest(i, s):
                spread_root(i, s)
                spread_out(i, s)

            turns(act, step3, 9)
            sums_in(*LAST)
            extremes_in(*LAST)
            rest(*divmod(GROUPS - 2, SLOTS))
            scaled(*LAST)
            rest(*LAST)

        @block.vector
        def _(dve):
            V = nc.vector
            V.memset(dsti[:, :], FAR).then_inc(s_init, 1)
            V.memset(nexti[:, :], FAR).then_inc(s_init, 1)
            V.memset(previ[:, :], -1).then_inc(s_init, 1)
            V.memset(one_col[:, :], 1.0)
            V.memset(eps_col[:, :], EPS)
            V.memset(srci[:, :], 0).then_inc(s_init, 1)
            V.memset(ones[:, :], 1.0).then_inc(s_init, 1)
            V.memset(sign[0:D, :], 1.0)
            V.memset(sign[D:P, :], -1.0)
            V.memset(weT[:, 0:D], 0.0)
            V.memset(coef[:, :], 0.0)
            V.memset(brow[:, :, :], 0.0)
            for b in L:
                for s in range(2):
                    V.memset(b["dT"][s % 2][D:D + 1, :], 1.0)
                    V.memset(b["S"][s % 2][D:D + 1, :], 1.0)
            chain = Order(dve, s_wready, 0)
            chain.begin(0)
            link = chain.link
            link(V.memset(carry[:, :], 0.0))
            dve.wait_ge(s_ld, 16 * len(loads))
            link(V.tensor_tensor(keep[:, :], dsti[:, :], previ[:, :], ALU.is_equal))
            link(V.tensor_tensor(same_next[:, :], dsti[:, :], nexti[:, :], ALU.is_equal))
            V.tensor_copy(masks_b[:, 0, :], keep[:, :])
            V.tensor_scalar(masks_b[:, 1, :], keep[:, :], -1.0, -LOW, ALU.add, ALU.mult)
            V.tensor_copy(rec_all[:, :, 0], srci[:, :])
            V.tensor_scalar(rec_all[:, :, 1], dsti[:, :], float(N - 1), None, ALU.min)
            V.scalar_tensor_tensor(sidx_all[:, :], same_next[:, :], float(FAR), dsti[:, :], ALU.mult, ALU.add)
            rec_f = rec_all[:, :, :].bitcast(F32)
            link(V.tensor_scalar(part_i[:, :], dsti[:, :], P - 1, None, ALU.bitwise_and))
            link(V.tensor_copy(rec_f[:, :, 2], part_i[:, :]))
            link(V.tensor_scalar(part_i[:, :], dsti[:, :], P.bit_length() - 1, None, ALU.logical_shift_right))
            link(V.tensor_copy(rec_f[:, :, 3], part_i[:, :]))
            link(V.tensor_scalar(part_i[:, :], srci[:, :], P * CHUNKS - 1, None, ALU.bitwise_and))
            link(V.tensor_copy(low512_all[:, :], part_i[:, :]))
            link(V.tensor_scalar(part_i[:, :], srci[:, :], (P * CHUNKS).bit_length() - 1, None,
                                 ALU.logical_shift_right))
            V.tensor_copy(rec_f[:, :, 4], part_i[:, :]).then_inc(s_recready, 1)
            dve.wait_ge(s_wld, 16 * len(wloads))
            dve.wait_ge(s_pe, 1)
            V.tensor_copy(weT[:, D:P], ps[0:D, 0, 0:D])
            V.tensor_copy(wpdT[:, :], ps[0:D, 0, D:2 * D])
            V.tensor_copy(wpxT[:, :], ps[0:D, 0, 2 * D:3 * D])
            V.tensor_copy(wpsT[:, 0:3, :].rearrange("p a f -> p (a f)"), ps[0:D, 1, 0:3 * P])
            V.tensor_copy(wpsT[:, 3:6, :].rearrange("p a f -> p (a f)"), ps[0:D, 2, 0:3 * P])
            link(V.tensor_tensor(wsum[:, :, :], wsh[:, :, MEAN, :], wsh[:, :, MIN, :], ALU.add))
            V.tensor_tensor(wsum[:, :, :], wsum[:, :, :], wsh[:, :, MAX, :], ALU.add).then_inc(s_dv, 1)
            dve.wait_ge(s_ac, 3)
            link(V.tensor_copy(hist[:, :], hist_i[:, :]))
            link(V.tensor_tensor(hl[:, :], hist[:, :], logb[:, :], ALU.mult))
            link(V.tensor_reduce(avg[:, 0:1], hl[:, :], AX, ALU.add))
            link(V.tensor_reduce(avg[:, 1:2], hist[:, :], AX, ALU.add))
            link(V.reciprocal(avg[:, 2:3], avg[:, 1:2]))
            link(V.tensor_tensor(avg[:, 3:4], avg[:, 0:1], avg[:, 2:3], ALU.mult))
            link(V.reciprocal(avg[:, 4:5], avg[:, 3:4]))
            link(V.reciprocal(avg[:, 5:6], two_col[:, 0:1]))
            link(V.tensor_copy(coef[D:P, 0:1], two_col[D:P, 1:2]))
            link(V.tensor_tensor(avg[:, 6:7], two_col[:, 0:1], avg[:, 4:5], ALU.mult))
            link(V.tensor_tensor(avg[:, 7:8], avg[:, 3:4], avg[:, 5:6], ALU.mult))
            link(V.tensor_tensor(coef[D:P, 1:2], avg[D:P, 6:7], two_col[D:P, 1:2], ALU.mult))
            link(V.tensor_tensor(coef[D:P, 2:3], avg[D:P, 7:8], two_col[D:P, 1:2], ALU.mult))
            dve.wait_ge(s_pe, 2)
            V.tensor_copy(wshT[:, :, :].rearrange("p a f -> p (a f)"), ps[0:D, 3, 0:3 * D])
            V.tensor_tensor(wshTx[:, :], ps[0:D, 3, 0:D], wpxT[:, :], ALU.add)
            link(V.tensor_tensor(bias2[:, :], ps[:, 4, 0:1], bpre2[:, :], ALU.add))
            V.tensor_tensor(sbias2[:, :], bias2[:, :], sign[:, :], ALU.mult)
            for a in range(2):
                V.tensor_copy(wcat[D:P, a, :], ps[D:P, 4, D:2 * D])
            V.tensor_copy(f_ms[:, :], ps[:, 5, 0:3 * D])
            V.tensor_scalar(f_xn[:, :], ps[:, 6, 0:3 * D], sign[:, :], None, ALU.mult)
            V.tensor_scalar(b1relu[:, :], b1row[:, :], 0.0, None, ALU.max)
            V.tensor_tensor(brow[:, 0, :], ps[0:1, 7, 0:D], blin_row[:, :], ALU.add).then_inc(s_dv, 1)
            V.tensor_tensor_scan(cnt[:, :], keep[:, :], ones[0:R, 0:GROUP], 0.0, ALU.mult, ALU.add)
            V.tensor_tensor_scan(whole[:, :], keep[:, :], keep[:, :], 1.0, ALU.mult, ALU.mult).then_inc(s_dv, 1)
            dve.wait_ge(s_pe, 4)
            V.tensor_copy(ends[:, 0, 0:R], ps[0:1, 3, 0:R])
            link(V.tensor_copy(ends[:, 1, 0:R], ps[0:1, 4, 0:R]))
            V.tensor_tensor_scan(carry[:, 1:R + 1], ends[:, 1, 0:R], ends[:, 0, 0:R], 0.0, ALU.mult,
                                 ALU.add).then_inc(s_dv, 1)
            V.tensor_copy(f_h[0:D, :], ps[0:D, 0, 0:3 * D])
            V.tensor_copy(w_dense[0:D, :], ps[0:D, 1, 0:D])
            V.tensor_tensor(crow[:, :], ps[0:1, 2, 0:D], brow[:, 0, :], ALU.add).then_inc(s_dv, 1)
            dve.wait_ge(s_pe, 5)
            link(V.tensor_copy(carry_col[:, :], ps[0:R, 5, 0:1]))

            def degrees(n):
                part = slice(GROUP // 4 * ((n - 1) % 4), GROUP // 4 * ((n - 1) % 4 + 1))
                if n == 0:
                    V.scalar_tensor_tensor(deg[:, :], whole[:, :], carry_col[:, :], cnt[:, :], ALU.mult,
                                           ALU.add).then_inc(s_fready, 1)
                elif n <= 4:
                    dve.wait_ge(s_fready, 1)
                    V.reciprocal(frec_all[:, part, 0], deg[:, part])
                elif n <= 8:
                    dve.wait_ge(s_ac, 4)
                    V.reciprocal(rlogd[:, part], logd[:, part]).then_inc(s_fready, 1)
                elif n == 9:
                    dve.wait_ge(s_fready, 5)
                    V.tensor_scalar(frec_all[:, :, 1], logd[:, :], avg[0:R, 4:5], None, ALU.mult)
                    V.tensor_scalar(frec_all[:, :, 2], rlogd[:, :], avg[0:R, 3:4], None, ALU.mult).then_inc(s_fready, 1)

            def wide(t, n):
                return t.rearrange("p (k o) -> p k o", o=1).to_broadcast([P, n, D])

            def moments(o, b, rows, lo, n, g, first=None, second=None):
                hi = lo + n
                o.link(V.tensor_reduce(b["st"][:, 0, lo:hi], rows, AX, ALU.add))
                need(dve, b["squared" if b is not c else "sumsq_ready"], g)
                V.scalar_tensor_tensor(b["xc"][:, lo:hi, :], wide(b["st"][:, 0, lo:hi], n), -1.0 / D, rows,
                                       ALU.mult, ALU.add).then_inc(b["rows_read"], 1)
                if first:
                    first()
                if b is c:
                    dve.wait_ge(b["squared"], g + 1)
                    V.tensor_reduce(b["st"][:, 1, lo:hi], b["sq"][:, lo:hi, :], AX, ALU.add).then_inc(
                        b["sumsq_ready"], 1)
                if second:
                    second()
                dve.wait_ge(b["std_ready"], g + 1)
                o.link(V.reciprocal(b["st"][:, 3, lo:hi], b["st"][:, 2, lo:hi]))

            def scan12(b, i, s):
                g = SLOTS * i + s
                dve.wait_ge(b["hT_ready"], g + 1)
                dve.wait_ge(b["inputs_loaded"][s], 32 * (i + 1))
                need(dve, b["scanned"], g)
                need(dve, b["hop_product"], g - 1)
                state = b["S"][1 - s % 2][0:D, GROUP - 1:GROUP] if before(i, s) else 0.0
                V.tensor_tensor_scan(b["S"][s % 2][0:D, :], b["keep"][s][:, :], b["hT"][s % 2][:, :], state,
                                     ALU.mult, ALU.add).then_inc(b["scanned"], 1)

            def dense12(b, i, s):
                g = SLOTS * i + s
                dve.wait_ge(b["dense_product"], g + 1)
                need(dve, b["dense_stored"][s], 16 * i)
                V.tensor_tensor(b["o"][s][:, :, :], b["pO"][:, 0:TILES * D].rearrange("p (k f) -> p k f", f=D),
                                b["x8"][s][:, TILES:2 * TILES, :], ALU.add).then_inc(b["dense_ready"], 1)

            def biased(b, i, s):
                dve.wait_ge(b["inputs_loaded"][s], 32 * i + 32)
                dx = b["x8"][s][:, TILES:2 * TILES, :]
                V.tensor_tensor(dx, dx, b2all[:, :].rearrange("p (o f) -> p o f", o=1).to_broadcast([P, TILES, D]),
                                ALU.add).then_inc(biased_rows, 1)

            def one_hots(i, s, tiles):
                g = SLOTS * i + s
                b = L[0]
                dve.wait_ge(b["idx_loaded"][s], 16 * i + 16)
                for k in tiles:
                    need(dve, b["counted"], TILES * g + k + 1 - TILES)
                    V.tensor_scalar(hot_lo[k][:, :], iota_hi[:, 0:P], b["rec"][s][:, k, 2:3].bitcast(F32), None,
                                    ALU.is_equal)
                    V.tensor_scalar(hot_hi[k][:, :], iota_hi[:, :], b["rec"][s][:, k, 3:4].bitcast(F32), None,
                                    ALU.is_equal).then_inc(b["hot_ready"], 1)

            def one_hots_src(i, s):
                g = SLOTS * i + s
                q = L[1]
                dve.wait_ge(q["idx_loaded"][s], 32 * i + 32)
                need(dve, q["looked_up"], g - 1)
                for ch in range(CHUNKS):
                    ins = V.tensor_scalar(hot[s % 2][:, ch, :], q["low512"][s][:, :], row_of[:, ch:ch + 1], None,
                                          ALU.is_equal)
                ins.then_inc(q["hot_ready"], 1)

            def find(i, s):
                g = SLOTS * i + s
                q = L[1]
                fo.begin(g)
                dve.wait_ge(q["looked_up"], g + 1)
                dve.wait_ge(q["idx_loaded"][s], 32 * i + 32)
                need(dve, q["rows_gathered"][s], TILES * 16 * i)
                need(dve, q["rows_saved"][s], 32 * i)
                need(dve, q["slots_found"], g)
                for k in range(TILES):
                    pick = V.scalar_tensor_tensor(pFound[:, k, 0:WIDE], iota_hi[:, 0:WIDE],
                                                  q["rec"][s][:, k, 4:5].bitcast(F32), pFound[:, k, 0:WIDE],
                                                  ALU.is_equal, ALU.mult, accum_out=slot_f[:, k:k + 1])
                fo.link(pick)
                V.tensor_copy(q["slots"][s][:, :], slot_f[:, :]).then_inc(q["slots_found"], 1)
                fo.end()

            fo = Order(dve, find_order, 1)

            for layer in (1, 2):
                b = L[layer - 1]
                o = Order(dve, norm_order, 2, 2 * GROUPS * (layer - 1))
                lo, n = (0, 2 * TILES) if layer == 1 else (TILES, TILES)

                def grow(i, s):
                    g = SLOTS * i + s
                    o.begin(g)
                    if not before(i, s):
                        biased(b, i, s)
                    dve.wait_ge(biased_rows, g + 1 + GROUPS * (layer - 1))
                    if layer == 1:
                        dve.wait_ge(b["rows_gathered"][s], TILES * 16 * (i + 1))
                    lower, higher = range(0, HALF), range(HALF, TILES)

                    def first():
                        if before(i, s, RESULT):
                            scan12(b, *before(i, s, RESULT))
                        if layer == 1:
                            one_hots(i, s, lower)

                    def second():
                        if before(i, s, RESULT):
                            dense12(b, *before(i, s, RESULT))
                        if layer == 1:
                            one_hots(i, s, higher)
                        if following(i, s):
                            biased(b, *following(i, s))

                    moments(o, b, b["x8"][s][:, lo:lo + n, :], lo, n, g, first, second)
                    need(dve, b["transposed"], g - 1)
                    V.scalar_tensor_tensor(b["h8"][s % 2][:, lo:lo + n, :], b["xc"][:, lo:lo + n, :], 0.0,
                                           wide(b["st"][:, 3, lo:lo + n], n), ALU.max, ALU.mult).then_inc(
                                               b["h_ready"], 1)
                    o.end()

                def step2(i, s):
                    one_hots_src(i, s)
                    if before(i, s, FOUND):
                        find(*before(i, s, FOUND))
                    if before(i, s, GROW):
                        grow(*before(i, s, GROW))
                    if isinstance(i, int) and SLOTS * i + s >= GROW:
                        degrees(SLOTS * i + s - GROW)

                if layer == 1:
                    turns(dve, grow, 9)
                    scan12(b, *before(*LAST))
                    to = Order(dve, s_wready, 8, chain.k)
                    to.begin(0)
                    halves = lambda t: t.rearrange("p (h n) -> p h n", h=2)
                    dve.wait_ge(b["counted"], TILES * GROUPS)
                    V.tensor_copy(halves(counts), pCount).then_inc(s_tab, 1)
                    scan12(b, *LAST)
                    dense12(b, *before(*LAST))
                    dve.wait_ge(s_tab, 1)
                    dve.wait_ge(b["transposed"], GROUPS)
                    V.tensor_scalar(filled, counts, 1.0, None, ALU.min)
                    dve.wait_ge(s_tabpe, 1)
                    for h in range(2):
                        state = incl[:, BANK - 1:BANK] if h else 0.0
                        cols = slice(h * BANK, (h + 1) * BANK)
                        to.link(V.tensor_tensor_scan(incl[:, cols], ones[:, cols], ps[:, 4 + h, 0:BANK], state,
                                                     ALU.mult, ALU.add))
                    to.link(V.tensor_tensor(halves(rank), halves(incl), ps[:, 4:6, 0:BANK], ALU.subtract))
                    to.link(V.scalar_tensor_tensor(halves(incl), halves(rank), -1.0 - DEFAULT, ps[:, 6:8, 0:BANK],
                                                   ALU.add, ALU.add))
                    to.link(V.tensor_tensor(counts, incl, filled, ALU.mult))
                    to.link(V.tensor_scalar(slot_i, counts, float(DEFAULT), None, ALU.add))
                    chunked = lambda t: t.rearrange("p (n c) -> p c n", c=CHUNKS)
                    to.link(V.tensor_scalar(slot_hi, slot_i, ~255, None, ALU.bitwise_and))
                    to.link(V.tensor_scalar(slot_lo, slot_i, 255, None, ALU.bitwise_and))
                    V.tensor_copy(table_hi[:, :, :], chunked(slot_hi))
                    V.tensor_copy(table_lo[:, :, :], chunked(slot_lo)).then_inc(s_tab, 1)
                    to.end()
                    dense12(b, *LAST)
                    dve.wait_ge(s_tab, 2)
                else:
                    turns(dve, step2, 13)
                    find(*LAST)
                    after_last(grow, GROW)
                    after_last(lambda i, s: scan12(b, i, s), RESULT)
                    after_last(lambda i, s: dense12(b, i, s), RESULT)

            oa = Order(dve, norm_order, 2, 4 * GROUPS)
            oc, od = Order(dve, c["order_c"], 1), Order(dve, c["order_d"], 2)

            def spread(i, s):
                g = SLOTS * i + s
                oc.begin(g)
                dve.wait_ge(c["moments_read"], g + 1)
                need(dve, c["spread_ready"], g - 1)
                oc.link(V.tensor_tensor(c["m2"][:, :, :], c["ms"][s % 2][:, :, D:2 * D], c["m2"][:, :, :],
                                        ALU.subtract))
                V.tensor_scalar(c["var"][s % 2][:, :, :], c["m2"][:, :, :], 0.0, EPS, ALU.max, ALU.add).then_inc(
                    c["var_ready"], 1)
                oc.end()

            def scan_sums(i, s):
                g = SLOTS * i + s
                dve.wait_ge(c["sums_in"], g + 1)
                dve.wait_ge(c["inputs_loaded"][s], 64 * i + 64)
                need(dve, c["scanned"], 2 * g)
                need(dve, c["back_done"], g - 1)
                V.tensor_tensor_scan(c["r1"][s % 2][:, :], c["masks"][s][:, 0, :], c["u1"][s % 2][:, :],
                                     c["r1"][1 - s % 2][:, GROUP - 1:GROUP] if before(i, s) else 0.0,
                                     ALU.mult, ALU.add).then_inc(c["scanned"], 1)

            def scan_extremes(i, s):
                g = SLOTS * i + s
                dve.wait_ge(c["msg_ready"], g + 1)
                need(dve, c["final_done"], g - SLOTS + 1)
                V.tensor_tensor_scan(c["r2"][s][:, :], c["masks"][s][:, 1, :], c["u2"][s % 2][:, :],
                                     c["r2"][s - 1][:, GROUP - 1:GROUP] if before(i, s) else LOW,
                                     ALU.add, ALU.max).then_inc(c["scanned"], 1)

            def final(i, s):
                g = SLOTS * i + s
                od.begin(g)
                dve.wait_ge(c["final_done"], g + 1)
                need(dve, c["out_stored"][s], 64 * i)
                need(dve, c["out_ready"], g)
                od.link(V.tensor_tensor(c["t1"][:, :, :], pF[:, :, 2 * D:3 * D],
                                        c["frec"][s][:, :, 2:3].to_broadcast([P, TILES, D]), ALU.mult))
                for k in range(TILES):
                    ins = V.scalar_tensor_tensor(c["t2"][:, k, :], pF[:, k, D:2 * D], c["frec"][s][:, k, 1:2],
                                                 c["t1"][:, k, :], ALU.mult, ALU.add)
                od.link(ins)
                V.tensor_tensor(c["o"][s][:, :, :], pF[:, :, 0:D], c["t2"][:, :, :], ALU.add).then_inc(
                    c["out_ready"], 1)
                od.end()

            def step3(i, s):
                g = SLOTS * i + s
                oa.begin(g)
                dve.wait_ge(c["inputs_loaded"][s], 64 * i + 64)
                dve.wait_ge(c["hop2_gathered"][s], 64 * i + 64)
                need(dve, c["out_ready"], g - SLOTS + 1)
                V.tensor_tensor(c["x2"][s][:, :, :], c["x8"][s][:, :, :], c["y8"][s][:, :, :], ALU.add).then_inc(
                    c["summed"], 1)
                dve.wait_ge(c["summed"], g + 1)

                def first():
                    if before(i, s, SPREAD):
                        spread(*before(i, s, SPREAD))
                    if before(i, s, SCAN):
                        scan_sums(*before(i, s, SCAN))

                moments(oa, c, c["x2"][s][:, :, :], 0, 2 * TILES, g,
                        first, lambda: scan_extremes(*before(i, s, SCAN)) if before(i, s, SCAN) else None)
                need(dve, c["hdT_done"], g - 1)
                V.scalar_tensor_tensor(c["cat"][s % 2][:, :, 0:D], c["xc"][:, 0:TILES, :], 0.0,
                                       wide(c["st"][:, 3, 0:TILES], TILES), ALU.max, ALU.mult)
                V.scalar_tensor_tensor(c["hd"][s % 2][:, :, :], c["xc"][:, TILES:, :], 0.0,
                                       wide(c["st"][:, 3, TILES:], TILES), ALU.max, ALU.mult).then_inc(c["h_ready"], 1)
                oa.end()
                if before(i, s, FINISH):
                    final(*before(i, s, FINISH))

            turns(dve, step3, 9)
            spread(*divmod(GROUPS - 2, SLOTS))
            scan_sums(*LAST)
            scan_extremes(*LAST)
            final(*divmod(GROUPS - 3, SLOTS))
            spread(*LAST)
            after_last(final, 2)


_INS = ['x', 'src', 'dst', 'edge_attr_64', 'L0_gnn_W1', 'L0_gnn_b1', 'L0_gnn_W2', 'L0_gnn_b2', 'L1_gnn_deg_hist',
        'L1_gnn_W_e', 'L1_gnn_b_e', 'L1_gnn_W_pre', 'L1_gnn_b_pre', 'L1_gnn_W_post', 'L1_gnn_b_post',
        'L1_gnn_W_lin', 'L1_gnn_b_lin']


def kernel(**inputs):
    import numpy as _np
    import concourse.bacc as _bacc
    from concourse import mybir as _mybir
    from concourse.bass_utils import run_bass_kernel_spmd as _run

    nc = _bacc.Bacc("TRN2", target_bir_lowering=False, num_devices=1)
    arrays, args = {}, []
    for name in _INS:
        a = _np.ascontiguousarray(inputs[name])
        arrays[f"in_{name}_dram"] = a
        args.append(nc.dram_tensor(f"in_{name}_dram", a.shape, _mybir.dt.from_np(a.dtype), kind="ExternalInput").ap())
    args.append(nc.dram_tensor("out_0_dram", (N, D), _mybir.dt.float32, kind="ExternalOutput").ap())
    gnn(nc, *args)
    r = _run(nc, [arrays], core_ids=[0])
    return r.results[0]["out_0_dram"]
```
